# Optimizing a Trainium2 kernel written in Bass

```python
import numpy as np
import jax
import jax.numpy as jnp

def _softmax(x, axis=-1):
    return jax.nn.softmax(x, axis=axis)

def _gelu(x):
    return jax.nn.gelu(x, approximate=True)

def _silu(x):
    return jax.nn.silu(x)

def _sigmoid(x):
    return jax.nn.sigmoid(x)

def _layernorm(x, axis=-1, eps=1e-05):
    m = jnp.mean(x, axis=axis, keepdims=True)
    v = jnp.var(x, axis=axis, keepdims=True)
    return (x - m) / jnp.sqrt(v + eps)

def _scatter_add(tgt, idx, src, axis=0):
    return tgt.at[idx].add(src)

def _segment_sum(src, seg, n):
    return jax.ops.segment_sum(src, seg, n)
kernel_name = 'mk_gnn_ffn_d1_gnn_r32_81eb0f'

def setup_inputs(seed: int=0):
    np.random.seed(seed)
    _w = jnp.asarray

    def _rec_inputs():
        import jax
        import jax.numpy as jnp
        _gk = jax.random.key(seed)
        x = -0.0003713 + 1 * jax.random.normal(jax.random.fold_in(_gk, 1), (3125, 256), jnp.float32)
        _s = jax.random.randint(jax.random.fold_in(_gk, 2), (25000,), 0, 3125, jnp.int32)
        _d = jax.random.randint(jax.random.fold_in(_gk, 3), (25000,), 0, 3125, jnp.int32)
        _loop = jnp.arange(3125, dtype=jnp.int32)
        src = jnp.concatenate([_s, _d, _loop])
        dst = jnp.concatenate([_d, _s, _loop])
        _o = jnp.argsort(dst, stable=True)
        src = src[_o]
        dst = dst[_o]
        edge_weight = jax.random.uniform(jax.random.fold_in(_gk, 12), (53125,), jnp.float32, 0.0, 0.999998)
        return (x, src, dst, edge_weight)
    x, src, dst, edge_weight = _rec_inputs()

    def _L0_gnn_setup():
        import jax, jax.numpy as jnp
        import numpy as np
        EPS = 1e-05

        def _bn(x, gamma, beta):
            m = jnp.mean(x, axis=0)
            v = jnp.mean((x - m) ** 2, axis=0)
            return gamma * (x - m) * jax.lax.rsqrt(v + EPS) + beta

        def _hconv(x, src, dst, ew, w1, b1, w2, b2, g, b):
            h = jax.nn.relu(x @ w1 + b1)
            msg = ew[:, None] * h[src]
            agg = jax.ops.segment_sum(msg, dst, num_segments=x.shape[0])
            h = agg @ w2 + b2
            return jax.nn.relu(_bn(h, g, b))
        N, C, E = (50000, 256, 9375)
        key = jax.random.key(seed)
        ks = jax.random.split(key, 16)
        s = 1.0 / np.sqrt(C)
        inp = {'x': jax.random.normal(ks[0], (N, C), dtype=jnp.float32), 'hyperedge_index': jax.random.randint(ks[1], (2, E), 0, N, dtype=jnp.int32), 'hyperedge_weight': jax.random.uniform(ks[2], (E,), dtype=jnp.float32), 'c1_w1': jax.random.normal(ks[3], (C, C), dtype=jnp.float32) * s, 'c1_b1': jnp.zeros((C,), jnp.float32), 'c1_w2': jax.random.normal(ks[4], (C, C), dtype=jnp.float32) * s, 'c1_b2': jnp.zeros((C,), jnp.float32), 'c1_g': jnp.ones((C,), jnp.float32), 'c1_b': jnp.zeros((C,), jnp.float32), 'bn1_g': jnp.ones((C,), jnp.float32), 'bn1_b': jnp.zeros((C,), jnp.float32), 'c2_w1': jax.random.normal(ks[5], (C, C), dtype=jnp.float32) * s, 'c2_b1': jnp.zeros((C,), jnp.float32), 'c2_w2': jax.random.normal(ks[6], (C, C), dtype=jnp.float32) * s, 'c2_b2': jnp.zeros((C,), jnp.float32), 'c2_g': jnp.ones((C,), jnp.float32), 'c2_b': jnp.zeros((C,), jnp.float32), 'bn2_g': jnp.ones((C,), jnp.float32), 'bn2_b': jnp.zeros((C,), jnp.float32)}
        return inp
    _L0_gnn_all = _L0_gnn_setup()
    _L0_gnn_in = {k: v for k, v in _L0_gnn_all.items() if k in ('c1_w1', 'c1_b1', 'c1_w2', 'c1_b2', 'c1_g', 'c1_b', 'bn1_g', 'bn1_b', 'c2_w1', 'c2_b1', 'c2_w2', 'c2_b2', 'c2_g', 'c2_b', 'bn2_g', 'bn2_b')}
    del _L0_gnn_all

    def _L0_ffn_setup():
        import math
        import jax, jax.numpy as jnp
        import numpy as np
        CAPACITY_FACTOR = 1.25
        key = jax.random.key(seed)
        ks = jax.random.split(key, 5)
        B, L, D, F, E = (8, 256, 256, 1024, 8)
        h = jax.random.normal(ks[0], (B, L, D), dtype=jnp.float32)
        gate_w = jax.random.normal(ks[1], (D, E), dtype=jnp.float32) * 0.02
        gate_b = jnp.zeros((E,), dtype=jnp.float32)
        w1 = jax.random.normal(ks[2], (E, D, F), dtype=jnp.float32) * (1.0 / math.sqrt(D))
        b1 = jnp.zeros((E, F), dtype=jnp.float32)
        w2 = jax.random.normal(ks[3], (E, F, D), dtype=jnp.float32) * (1.0 / math.sqrt(F))
        b2 = jnp.zeros((E, D), dtype=jnp.float32)
        return {'h': h, 'gate_w': gate_w, 'gate_b': gate_b, 'w1': w1, 'b1': b1, 'w2': w2, 'b2': b2}
    _L0_ffn_all = _L0_ffn_setup()
    _L0_ffn_in = {k: v for k, v in _L0_ffn_all.items() if k in ('gate_w', 'gate_b', 'w1', 'b1', 'w2', 'b2')}
    del _L0_ffn_all
    return {'x': x, 'src': src, 'dst': dst, 'edge_weight': edge_weight, 'L0_gnn_c1_w1': _L0_gnn_in['c1_w1'], 'L0_gnn_c1_b1': _L0_gnn_in['c1_b1'], 'L0_gnn_c1_w2': _L0_gnn_in['c1_w2'], 'L0_gnn_c1_b2': _L0_gnn_in['c1_b2'], 'L0_gnn_c1_g': _L0_gnn_in['c1_g'], 'L0_gnn_c1_b': _L0_gnn_in['c1_b'], 'L0_gnn_bn1_g': _L0_gnn_in['bn1_g'], 'L0_gnn_bn1_b': _L0_gnn_in['bn1_b'], 'L0_gnn_c2_w1': _L0_gnn_in['c2_w1'], 'L0_gnn_c2_b1': _L0_gnn_in['c2_b1'], 'L0_gnn_c2_w2': _L0_gnn_in['c2_w2'], 'L0_gnn_c2_b2': _L0_gnn_in['c2_b2'], 'L0_gnn_c2_g': _L0_gnn_in['c2_g'], 'L0_gnn_c2_b': _L0_gnn_in['c2_b'], 'L0_gnn_bn2_g': _L0_gnn_in['bn2_g'], 'L0_gnn_bn2_b': _L0_gnn_in['bn2_b'], 'L0_ffn_gate_w': _L0_ffn_in['gate_w'], 'L0_ffn_gate_b': _L0_ffn_in['gate_b'], 'L0_ffn_w1': _L0_ffn_in['w1'], 'L0_ffn_b1': _L0_ffn_in['b1'], 'L0_ffn_w2': _L0_ffn_in['w2'], 'L0_ffn_b2': _L0_ffn_in['b2']}

def reference(x, src, dst, edge_weight, L0_gnn_c1_w1, L0_gnn_c1_b1, L0_gnn_c1_w2, L0_gnn_c1_b2, L0_gnn_c1_g, L0_gnn_c1_b, L0_gnn_bn1_g, L0_gnn_bn1_b, L0_gnn_c2_w1, L0_gnn_c2_b1, L0_gnn_c2_w2, L0_gnn_c2_b2, L0_gnn_c2_g, L0_gnn_c2_b, L0_gnn_bn2_g, L0_gnn_bn2_b, L0_ffn_gate_w, L0_ffn_gate_b, L0_ffn_w1, L0_ffn_b1, L0_ffn_w2, L0_ffn_b2):
    import jax
    import jax.numpy as jnp

    def _L0_gnn_ref(x, hyperedge_index, hyperedge_weight, c1_w1, c1_b1, c1_w2, c1_b2, c1_g, c1_b, bn1_g, bn1_b, c2_w1, c2_b1, c2_w2, c2_b2, c2_g, c2_b, bn2_g, bn2_b):
        import jax, jax.numpy as jnp
        import numpy as np
        EPS = 1e-05

        def _bn(x, gamma, beta):
            m = jnp.mean(x, axis=0)
            v = jnp.mean((x - m) ** 2, axis=0)
            return gamma * (x - m) * jax.lax.rsqrt(v + EPS) + beta

        def _hconv(x, src, dst, ew, w1, b1, w2, b2, g, b):
            h = jax.nn.relu(x @ w1 + b1)
            msg = ew[:, None] * h[src]
            agg = jax.ops.segment_sum(msg, dst, num_segments=x.shape[0])
            h = agg @ w2 + b2
            return jax.nn.relu(_bn(h, g, b))
        src, dst = (hyperedge_index[0], hyperedge_index[1])
        residual = x
        h = _hconv(x, src, dst, hyperedge_weight, c1_w1, c1_b1, c1_w2, c1_b2, c1_g, c1_b)
        h = jax.nn.relu(_bn(h, bn1_g, bn1_b))
        h = _hconv(h, src, dst, hyperedge_weight, c2_w1, c2_b1, c2_w2, c2_b2, c2_g, c2_b)
        h = _bn(h, bn2_g, bn2_b)
        return jax.nn.relu(h + residual)

    def _L0_ffn_ref(h, gate_w, gate_b, w1, b1, w2, b2):
        import math
        import jax, jax.numpy as jnp
        import numpy as np
        CAPACITY_FACTOR = 1.25
        B, L, D = h.shape
        E = gate_w.shape[1]
        T = B * L
        C = max(1, math.ceil(CAPACITY_FACTOR * T / E))
        x = h.reshape(T, D)
        logits = x @ gate_w + gate_b
        probs = jax.nn.softmax(logits, axis=-1)
        idx = jnp.argmax(probs, axis=-1)
        prb = jnp.take_along_axis(probs, idx[:, None], axis=1)[:, 0]
        one_hot = jax.nn.one_hot(idx, E, dtype=jnp.float32)
        pos = (jnp.cumsum(one_hot, axis=0) * one_hot).sum(-1).astype(jnp.int32) - 1
        kept = pos < C
        pos_safe = jnp.where(kept, pos, C)
        buf = jnp.zeros((E, C, D), dtype=h.dtype).at[idx, pos_safe].set(x, mode='drop')
        hmid = jax.nn.relu(jnp.einsum('ecd,edf->ecf', buf, w1) + b1[:, None, :])
        ybuf = jnp.einsum('ecf,efd->ecd', hmid, w2) + b2[:, None, :]
        pos_g = jnp.minimum(pos, C - 1)
        y_tok = ybuf[idx, pos_g] * (prb * kept)[:, None]
        y = y_tok.reshape(B, L, D)
        y = jnp.nan_to_num(y, nan=0.0, posinf=10000.0, neginf=-10000.0)
        return y
    edge_index = jnp.stack([src, dst])
    x = x + _L0_gnn_ref(_layernorm(x, axis=-1), edge_index, edge_weight, L0_gnn_c1_w1, L0_gnn_c1_b1, L0_gnn_c1_w2, L0_gnn_c1_b2, L0_gnn_c1_g, L0_gnn_c1_b, L0_gnn_bn1_g, L0_gnn_bn1_b, L0_gnn_c2_w1, L0_gnn_c2_b1, L0_gnn_c2_w2, L0_gnn_c2_b2, L0_gnn_c2_g, L0_gnn_c2_b, L0_gnn_bn2_g, L0_gnn_bn2_b)
    x = x + _L0_ffn_ref(_layernorm(x, axis=-1)[None], L0_ffn_gate_w, L0_ffn_gate_b, L0_ffn_w1, L0_ffn_b1, L0_ffn_w2, L0_ffn_b2)[0]
    return x

_drawn_inputs = setup_inputs


def setup_inputs(seed=0):
    import zlib

    import numpy as np

    out = dict(_drawn_inputs(seed))
    spreads = {'L0_gnn_c1_b1': (0.0, 0.1),
     'L0_gnn_c1_b2': (0.0, 0.8),
     'L0_gnn_c1_g': (1.0, 0.6),
     'L0_gnn_c1_b': (0.0, 0.287),
     'L0_gnn_bn1_g': (1.0, 0.2),
     'L0_gnn_bn1_b': (0.0, 0.1),
     'L0_gnn_c2_b1': (0.0, 0.1),
     'L0_gnn_c2_b2': (0.0, 0.8),
     'L0_gnn_c2_g': (1.0, 0.6),
     'L0_gnn_c2_b': (0.0, 0.277),
     'L0_gnn_bn2_g': (1.0, 0.2),
     'L0_gnn_bn2_b': (0.0, 0.1),
     'L0_ffn_gate_b': (0.0, 0.1),
     'L0_ffn_b1': (0.0, 0.8),
     'L0_ffn_b2': (0.0, 0.76)}
    factors = {}
    for name, (base, spread) in spreads.items():
        noise = np.random.default_rng([zlib.crc32(name.encode()), seed]).standard_normal(out[name].shape)
        drawn = base * np.exp(spread * noise) if base else spread * noise
        out[name] = jnp.asarray(drawn.astype(out[name].dtype))
    for name, factor in factors.items():
        out[name] = (out[name] * factor).astype(out[name].dtype)
    return out
```

```python
from contextlib import ExitStack

import numpy as np

import concourse.bass as bass
from concourse import mybir

F32 = mybir.dt.float32
I32 = mybir.dt.int32
U32 = mybir.dt.uint32
ALU = mybir.AluOpType
ACT = mybir.ActivationFunctionType
AX_X = mybir.AxisListType.X

P = 128
EPS = 1e-5
FLT_MAX = float(np.finfo(np.float32).max)
NAN_TO_NUM_INF = 1e4


def gnn_moe_program(nc, x, src, dst, ew, conv, gate_w, gate_b, w1, b1, w2, b2, out):
    N, D = x.shape
    (E,) = src.shape
    NE, _, F = w1.shape
    H = D // P
    TILES = -(-N // P)
    TAIL = N - (TILES - 1) * P
    NPAD = TILES * P
    CHUNKS = -(-E // P)
    GROUPS = -(-CHUNKS // P)
    CROSS = TILES - 1
    BLOCK = 8
    GROUP = 4
    BODY = 2 * BLOCK
    ITER = CHUNKS // BODY
    BLOCKS = CHUNKS // BLOCK
    NGROUP = CHUNKS // GROUP
    XGROUP = CROSS // GROUP
    assert CROSS <= 24 and 96 + CHUNKS <= 512
    assert CHUNKS % BODY == 0 and CROSS % GROUP == 0 and H == 2
    NB = -(-N // 512)
    EARLY = [-(-(CHUNKS * 512 * (j + 1) // N + 10) // BODY) for j in range(NB)]
    EARLY = [i for i in EARLY if i <= ITER - 3]
    FT = F // P
    CAP = max(1, -(-5 * N // (4 * NE)))
    ESLOT = 512
    ST = ESLOT // P
    ROW = 2 * D + 2
    FAR = 1 << 20
    assert CAP <= ESLOT
    XG = [(0, 6), (6, 12), (12, 18), (18, TILES)]

    h_dram = [nc.dram_tensor(f"h{l}", (N, D), F32, kind="Internal").ap() for l in range(2)]
    ebuf = nc.dram_tensor("expert_rows", (NE * ESLOT, ROW), F32, kind="Internal").ap()

    with ExitStack() as ctx:
        def sb(name, shape, dt=F32):
            return ctx.enter_context(nc.sbuf_tensor(name, shape, dt))

        def sem(name):
            return ctx.enter_context(nc.semaphore(name))

        rows = sb("rows", [P, TILES, ROW])
        xnT = sb("xnT", [P, H, NPAD])
        aggT = sb("aggT", [P, H, NPAD + P])
        zT = sb("zT", [P, H, NPAD])
        msgs = sb("msgs", [P, BODY, D])
        S = sb("S", [P, 2 * GROUP, P])
        edges = aggT[:, :, :].rearrange("p h n -> p (h n)")
        GE = GROUPS * P
        metaI = edges[:, 0:2 * GE].bitcast(I32).rearrange("p (k g e) -> p k g e", k=2, e=P)
        metaF = edges[:, 2 * GE:5 * GE].rearrange("p (k g e) -> p k g e", k=3, e=P)
        relT = edges[:, 5 * GE:6 * GE].rearrange("p (g e) -> p g e", e=P)
        metaE = sb("metaE", [P, 3, CHUNKS + BLOCK])
        metaX = sb("metaX", [P, 3, CROSS])
        idx_x = sb("idx_x", [P, CROSS], I32)
        idx_now = sb("idx_now", [P, 2, BLOCK], I32)
        relw_now = sb("relw_now", [P, 2, 2, BLOCK])
        offs_f = sb("offs_f", [1, CHUNKS])
        offs = sb("offs", [1, CHUNKS], I32)
        late_f = sb("late_f", [1, NB + 1])
        late_i = sb("late_i", [1, 1], I32)
        iota_i = sb("iota_i", [P, P], I32)
        iota_f = sb("iota_f", [P, P])
        bound_i = sb("bound_i", [P, CROSS], I32)
        bound = sb("bound", [P, CROSS])
        gt_first, pick = (
            edges[:, 6 * GE + P + k * GROUPS * CROSS:6 * GE + P + (k + 1) * GROUPS * CROSS].rearrange("p (g u) -> p g u", g=GROUPS)
            for k in range(2))
        nfar = sb("nfar", [P, GROUPS])
        ident = sb("ident", [P, P])
        upper = sb("upper", [P, P])
        ones = sb("ones", [P, P])
        wc = sb("wc", [P, 2, 2, H, D])
        b1row = sb("b1row", [1, 2, D])
        colsrc = edges[:, 6 * GE:6 * GE + P]
        farW = edges[:, 7 * GE:8 * GE].rearrange("p (g e) -> p g e", e=P)
        far = edges[:, 8 * GE:9 * GE].rearrange("p (g e) -> p g e", e=P)
        cols = sb("cols", [P, P])
        gw = sb("gw", [P, H, NE])
        gb = sb("gb", [1, NE])
        we1 = sb("we1", [P, 2, H, F])
        we2 = sb("we2", [P, 2, FT, D])
        be2 = sb("be2", [1, 2, D])
        st = sb("st", [P, TILES, 6])
        mv = sb("mv", [P, TILES, 2])
        sd = sb("sd", [P, TILES])
        sq = sb("sq", [P, TILES])
        rs = sb("rs", [P, TILES])
        bst = sb("bst", [P, H, NB, 6])
        bmv = sb("bmv", [P, H, 2])
        bsd = sb("bsd", [P, H])
        bsq = sb("bsq", [P, H])
        brs = sb("brs", [P, H])
        bsc = sb("bsc", [P, H])
        bms = sb("bms", [P, H])
        bof = sb("bof", [P, H])
        lg, ex, hot, tot, cum = (
            xnT[:, 1, NPAD - (k + 1) * TILES * NE:NPAD - k * TILES * NE].rearrange("p (t e) -> p t e", e=NE) for k in range(5))
        rank_i = sb("rank_i", [P, NE], I32)
        rank = sb("rank", [P, NE])
        base_i = sb("base_i", [P, NE], I32)
        base = sb("base", [P, NE])
        r1 = sb("r1", [P, TILES])
        r2 = sb("r2", [P, TILES])
        r3 = sb("r3", [P, TILES])
        r4 = sb("r4", [P, TILES])
        tok_i = sb("tok_i", [P, TILES], I32)
        tok_f = sb("tok_f", [P, TILES])
        slot_i = sb("slot_i", [P, TILES], I32)

        xf, zf, af = (t[:, :, :].rearrange("p h n -> p (h n)") for t in (xnT, zT, aggT))
        hid = [b[:, 0:FT * ESLOT].rearrange("p (f s) -> p f s", f=FT) for b in (xf, zf)]
        inT = [b[:, FT * ESLOT:(FT + H) * ESLOT].rearrange("p (h s) -> p h s", h=H) for b in (xf, zf)]
        erow = [af[:, i * ST * ROW:(i + 1) * ST * ROW].rearrange("p (s r) -> p s r", s=ST) for i in range(2)]
        yv = af[:, 2 * ST * ROW:2 * ST * ROW + D]
        ymask = af[:, 2 * ST * ROW + D:2 * ST * ROW + 2 * D]
        ya = af[:, 2 * ST * ROW + 2 * D:2 * ST * ROW + 3 * D]
        yo = msgs[:, 0:4, :]
        fill = zT[:, 0, 0:ROW]

        bank = [ctx.enter_context(nc.psum_tensor(f"bank{i}", [P, 512], F32)) for i in range(8)]

        x_in = [sem(f"x_in{g}") for g in range(len(XG))]
        meta_zero = sem("meta_zero")
        meta_in = sem("meta_in")
        small_in = sem("small_in")
        consts = sem("consts")
        pads = sem("pads")
        tail_zero = sem("tail_zero")
        fill_ready = sem("fill_ready")
        filled = sem("filled")
        dve_chain = sem("dve_chain")
        meta_f = sem("meta_f")
        meta_rel = sem("meta_rel")
        pe_meta = sem("pe_meta")
        metaE_done = sem("metaE_done")
        var_ready = sem("var_ready")
        sqrt_done = sem("sqrt_done")
        rows_norm = sem("rows_norm")
        pe_tr = sem("pe_tr")
        tr_out = sem("tr_out")
        pe_h = sem("pe_h")
        h_out = sem("h_out")
        h_stored = sem("h_stored")
        staged = sem("staged")
        pool_go = sem("pool_go")
        got = [sem(f"got{j}") for j in range(BODY)]
        s_ready = sem("s_ready")
        p_ready = sem("p_ready")
        late_ready = sem("late_ready")
        pe_far = sem("pe_far")
        x_got = sem("x_got")
        x_s = sem("x_s")
        x_p = sem("x_p")
        x_acc = sem("x_acc")
        x_z = sem("x_z")
        x_zout = sem("x_zout")
        acc_done = sem("acc_done")
        pe_z = sem("pe_z")
        z_out = sem("z_out")
        bvar_ready = sem("bvar_ready")
        bsqrt_done = sem("bsqrt_done")
        coef_ready = sem("coef_ready")
        y_out = sem("y_out")
        act_in = sem("act_in")
        res_mul = sem("res_mul")
        pe_back = sem("pe_back")
        x1_ready = sem("x1_ready")
        pe_gate = sem("pe_gate")
        lg_ready = sem("lg_ready")
        exp_done = sem("exp_done")
        hot_ready = sem("hot_ready")
        pe_rank = sem("pe_rank")
        slots_ready = sem("slots_ready")
        x1_stored = sem("x1_stored")
        dispatched = sem("dispatched")
        w_in = [sem(f"w_in{i}") for i in range(2)]
        erow_in = [sem(f"erow_in{i}") for i in range(2)]
        pe_in = sem("pe_in")
        in_out = sem("in_out")
        pe_hid = sem("pe_hid")
        hid_out = sem("hid_out")
        pe_y = sem("pe_y")
        y_read = sem("y_read")
        y_ready = sem("y_ready")
        y_sent = [sem(f"y_sent{i}") for i in range(4)]

        def expert_bias(e, f):
            return cols[:, e * FT + f:e * FT + f + 1]

        B2, G, B, BNG, BNB = range(5)
        VEC = NE * FT

        def vec(l, which, h=None):
            c = VEC + (l * 5 + which) * H
            return cols[:, c:c + H] if h is None else cols[:, c + h:c + h + 1]

        PAIRS = [(2 * j, min(2, TILES - 2 * j)) for j in range(-(-TILES // 2))]
        NP = len(PAIRS)
        WIDTH = [min(512, N - 512 * j) for j in range(NB)]
        ACC = GROUP + CHUNKS

        block = ctx.enter_context(nc.Block())

        @block.sync
        def _(sp):
            xt = x[0:(TILES - 1) * P, :].rearrange("(t p) d -> p t d", p=P)
            for g, (a, b) in enumerate(XG):
                if b == TILES:
                    sp.wait_ge(tail_zero, 1)
                    sp.dma_start(rows[0:TAIL, TILES - 1, D:2 * D], x[(TILES - 1) * P:, :]).then_inc(x_in[g], 16)
                    b -= 1
                sp.dma_start(rows[:, a:b, D:2 * D], xt[:, a:b, :]).then_inc(x_in[g], 16)
            whole, rest = CHUNKS - 1 - (GROUPS - 1) * P, E - (CHUNKS - 1) * P
            sp.wait_ge(meta_zero, 4)
            for ap, to in ((src, metaI[:, 0]), (dst, metaI[:, 1]), (ew, metaF[:, 2])):
                g3, cut = (GROUPS - 1) * P * P, (CHUNKS - 1) * P
                sp.dma_start(to[:, 0:GROUPS - 1, :], ap[0:g3].rearrange("(g c e) -> c g e", c=P, e=P)).then_inc(meta_in, 16)
                sp.dma_start(to[0:whole, GROUPS - 1, :], ap[g3:cut].rearrange("(c e) -> c e", e=P)).then_inc(meta_in, 16)
                sp.dma_start(to[whole:whole + 1, GROUPS - 1, 0:rest], ap[cut:E].rearrange("(c e) -> c e", c=1)).then_inc(meta_in, 16)
            def load_expert(e):
                sp.dma_start(we1[:, e % 2], w1[e].rearrange("(h p) f -> p h f", p=P)).then_inc(w_in[e % 2], 16)
                sp.dma_start(we2[:, e % 2], w2[e].rearrange("(f p) n -> p f n", p=P)).then_inc(w_in[e % 2], 16)
                sp.dma_start(be2[:, e % 2, :], b2[e:e + 1, :]).then_inc(w_in[e % 2], 16)

            for l in range(2):
                ht = h_dram[l][0:(TILES - 1) * P, :].rearrange("(t p) d -> p t d", p=P)
                for a, b in XG:
                    sp.wait_ge(h_out, l * NP + -(-b // 2))
                    if b == TILES:
                        b -= 1
                        sp.dma_start(h_dram[l][b * P:, :], rows[0:TAIL, b, 0:D]).then_inc(h_stored, 16)
                    sp.dma_start(ht[:, a:b, :], rows[:, a:b, 0:D]).then_inc(h_stored, 16)
                if l == 0:
                    sp.wait_ge(fill_ready, 2)
                    for i in range(NE * ST):
                        sp.dma_start(ebuf[i * P:(i + 1) * P, :], fill).then_inc(filled, 16)
                    load_expert(0)
                    load_expert(1)
            ot = out[0:(TILES - 1) * P, :].rearrange("(t p) d -> p t d", p=P)
            for a, b in XG:
                sp.wait_ge(x1_ready, -(-b // 2))
                if b == TILES:
                    b -= 1
                    sp.dma_start(out[b * P:, :], rows[0:TAIL, b, D:2 * D]).then_inc(x1_stored, 16)
                sp.dma_start(ot[:, a:b, :], rows[:, a:b, D:2 * D]).then_inc(x1_stored, 16)
            sp.wait_ge(dispatched, 16 * TILES)
            for e in range(NE):
                if e >= 2:
                    sp.wait_ge(y_ready, ST * (e - 1))
                    for i in range(4):
                        sp.wait_ge(y_sent[i], 16 * (e - 1))
                sp.dma_start(erow[e % 2], ebuf[e * ESLOT:(e + 1) * ESLOT, :].rearrange("(s p) r -> p s r", p=P)).then_inc(erow_in[e % 2], 16)
                if e >= 2:
                    load_expert(e)
            for i in range(4):
                sp.wait_ge(y_sent[i], 16 * (NE * ST // 4))

        @block.gpsimd
        def _(pool):
            nc.gpsimd.memset(metaI[:, 0, GROUPS - 1, :], 0).then_inc(meta_zero, 1)
            nc.gpsimd.memset(metaI[:, 1, GROUPS - 1, :], NPAD + P).then_inc(meta_zero, 1)
            nc.gpsimd.memset(metaF[:, 2, GROUPS - 1, :], 0.0).then_inc(meta_zero, 1)
            nc.gpsimd.memset(colsrc, 0.0).then_inc(meta_zero, 1)
            nc.gpsimd.iota(iota_i[:, :], [[1, P]], base=0, channel_multiplier=0).then_inc(consts, 1)
            nc.gpsimd.iota(bound_i[:, :], [[P, CROSS]], base=P, channel_multiplier=0).then_inc(consts, 1)
            nc.gpsimd.iota(rank_i[:, :], [[-1, NE]], base=NE, channel_multiplier=0).then_inc(consts, 1)
            nc.gpsimd.iota(base_i[:, :], [[ESLOT, NE]], base=0, channel_multiplier=0).then_inc(consts, 1)
            nc.gpsimd.iota(tok_i[:, :], [[P, TILES]], base=0, channel_multiplier=1).then_inc(consts, 1)
            nc.gpsimd.memset(ident[:, :], 0.0).then_inc(consts, 1)
            nc.gpsimd.memset(upper[:, :], 1.0).then_inc(consts, 1)
            nc.gpsimd.memset(ones[:, :], 1.0).then_inc(consts, 1)
            pool.wait_ge(consts, 8)
            nc.gpsimd.affine_select(out=ident[:, :], in_=ident[:, :], compare_op=ALU.not_equal, fill=1.0, base=0,
                                    pattern=[[-1, P]], channel_multiplier=1).then_inc(consts, 1)
            nc.gpsimd.affine_select(out=upper[:, :], in_=upper[:, :], compare_op=ALU.is_ge, fill=0.0, base=0,
                                    pattern=[[1, P]], channel_multiplier=-1).then_inc(consts, 1)
            nc.gpsimd.memset(fill, 0.0).then_inc(fill_ready, 1)
            pool.wait_ge(fill_ready, 1)
            nc.gpsimd.memset(fill[:, 2 * D:2 * D + 1].bitcast(I32), FAR).then_inc(fill_ready, 1)
            nc.gpsimd.memset(metaE[:, :, CHUNKS:], 0.0).then_inc(pads, 1)
            nc.gpsimd.memset(zT[:, :, N:], 0.0).then_inc(pads, 1)

            late = None
            for l in range(2):
                pool.wait_ge(h_stored, 16 * 5 * (l + 1))
                with pool.Fori(0, ITER, 1) as i:
                    for b in range(2):
                        pool.wait_ge(staged, i * 2 + (l * (BLOCKS + 1) + b + 1))
                        pool.sem_inc(pool_go, 1)
                        for k in range(BLOCK):
                            nc.gpsimd.indirect_dma_start(
                                out=msgs[:, b * BLOCK + k, :], out_offset=None, in_=h_dram[l],
                                in_offset=bass.IndirectOffsetOnAxis(ap=idx_now[:, b, k:k + 1], axis=0),
                            ).then_inc(got[b * BLOCK + k], 16)
                if late is None:
                    pool.wait_ge(late_ready, 1)
                    late = pool.value_load(late_i[0:1, 0:1], min_val=0, max_val=E + NB)
                with pool.If(late > 0):
                    pool.wait_ge(acc_done, (l + 1) * ACC)
                    for u in range(CROSS):
                        if u >= BODY and u % GROUP == 0:
                            pool.wait_ge(x_acc, l * CROSS + u - BODY + GROUP)
                        nc.gpsimd.indirect_dma_start(
                            out=msgs[:, u % BODY, :], out_offset=None, in_=h_dram[l],
                            in_offset=bass.IndirectOffsetOnAxis(ap=idx_x[:, u:u + 1], axis=0),
                        ).then_inc(x_got, 16)
                        if u % GROUP == GROUP - 1:
                            pool.wait_ge(x_got, 16 * (l * CROSS + u + 1))
            pool.wait_ge(filled, 16 * NE * ST)
            pool.wait_ge(slots_ready, 1)
            for t in range(TILES):
                nc.gpsimd.indirect_dma_start(
                    out=ebuf, out_offset=bass.IndirectOffsetOnAxis(ap=slot_i[:, t:t + 1], axis=0),
                    in_=rows[:, t, :], in_offset=None, bounds_check=NE * ESLOT - 1, oob_is_err=False,
                ).then_inc(dispatched, 16)
            pool.wait_ge(x1_stored, 16 * 5)
            for i in range(NE * ST):
                e, s = divmod(i, ST)
                pool.wait_ge(y_ready, i + 1)
                nc.gpsimd.indirect_dma_start(
                    out=out, out_offset=bass.IndirectOffsetOnAxis(ap=erow[e % 2][:, s, 2 * D:2 * D + 1].bitcast(I32), axis=0),
                    in_=yo[:, i % 4, :], in_offset=None, bounds_check=N - 1, oob_is_err=False,
                ).then_inc(y_sent[i % 4], 16)

        @block.tensor
        def _(pe):
            pe.wait_ge(consts, 10)

            def rows_to_T(n, j):
                t, w = PAIRS[j]
                pe.wait_ge(rows_norm, n * TILES + t + w)
                if j >= 2:
                    pe.wait_ge(tr_out, n * NP + j - 1)
                for h in range(H):
                    for k in range(w):
                        mm = nc.tensor.transpose(bank[6 + j % 2][:, h * 256 + k * P:h * 256 + (k + 1) * P],
                                                 rows[:, t + k, h * P:(h + 1) * P], ident[:, :])
                mm.then_inc(pe_tr, 1)

            def h_rows(l, j):
                t, w = PAIRS[j]
                if l == 0:
                    pe.wait_ge(tr_out, j + 1)
                else:
                    pe.wait_ge(act_in, min(NB, -(-(t + w) * P // 512)) * H)
                if j >= 2:
                    pe.wait_ge(h_out, l * NP + j - 1)
                for k in range(w):
                    o = bank[4 + j % 2][:, k * D:(k + 1) * D]
                    for h in range(H):
                        nc.tensor.matmul(o, (xnT, zT)[l][:, h, (t + k) * P:(t + k + 1) * P], wc[:, l, 0, h, :], start=(h == 0), stop=False)
                    mm = nc.tensor.matmul(o, ones[0:1, :], b1row[:, l, :], start=False, stop=True)
                mm.then_inc(pe_h, 1)

            def z_block(j, fo, b):
                for h in range(H):
                    mm = nc.tensor.matmul(bank[b][:, 0:WIDTH[j]], wc[:, l, 1, h, fo * P:(fo + 1) * P],
                                          aggT[:, h, 512 * j:512 * j + WIDTH[j]], start=(h == 0), stop=(h == H - 1))
                return mm

            pe.wait_ge(meta_rel, 1)
            for k in range(3):
                for g in range(GROUPS):
                    a = relT[:, g, :] if k == 1 else metaF[:, k, g, :]
                    mm = nc.tensor.transpose(bank[k][:, g * P:(g + 1) * P], a, ident[:, :])
            for k in range(3):
                for g in range(GROUPS):
                    a = farW[:, g, :] if k == 2 else metaF[:, k, g, :]
                    mm = nc.tensor.matmul(bank[3][:, k * 32:k * 32 + CROSS], a, pick[:, g, :],
                                          start=(g == 0), stop=(g == GROUPS - 1))
            for g in range(GROUPS):
                nc.tensor.matmul(bank[3][0:1, 24:25], nfar[:, g:g + 1], ones[:, 0:1], start=(g == 0), stop=(g == GROUPS - 1))
            for g in range(GROUPS):
                nc.tensor.matmul(bank[3][0:1, 96 + g * P:min(96 + (g + 1) * P, 512)], metaF[:, 1, g, 0:1], ident[:, 0:min(P, CHUNKS - g * P)], start=True, stop=True)
            pe.wait_ge(small_in, 16 * 19)
            nc.tensor.transpose(bank[5][:, 0:P], colsrc, ident[:, :]).then_inc(pe_meta, 1)
            for j in range(NP + 2):
                if j < NP:
                    rows_to_T(0, j)
                if j == 2:
                    pe.wait_ge(metaE_done, 4)
                if j >= 2:
                    h_rows(0, j - 2)
            late = None
            for l in range(2):
                if l:
                    for j in range(NP):
                        h_rows(1, j)
                for n, (a, b) in enumerate(zip([0] + EARLY, EARLY + [ITER])):
                    with pe.Fori(a, b, 1) as i:
                        for q in range(4):
                            pe.wait_ge(s_ready, i * 4 + (l * (NGROUP + 1) + q + 1))
                            pe.wait_ge(acc_done, i * (4 * GROUP) + (l * ACC + q * GROUP))
                            for k in range(GROUP):
                                j = q * GROUP + k
                                pe.wait_ge(got[j], i * 16 + 16 * (l * ITER + 1))
                                o = bank[2 * (q % 2) + k // 2]
                                for h in range(H):
                                    mm = nc.tensor.matmul(o[:, (k % 2) * 256 + h * P:(k % 2) * 256 + (h + 1) * P],
                                                          msgs[:, j, h * P:(h + 1) * P], S[:, (q % 2) * GROUP + k, :],
                                                          start=True, stop=True)
                            mm.then_inc(p_ready, 1)
                    if b < ITER:
                        pe.wait_ge(acc_done, l * ACC + GROUP + b * BODY)
                        for fo in range(H):
                            if n >= 2:
                                pe.wait_ge(z_out, l * NB * H + (n - 2) * H + fo + 1)
                            z_block(n, fo, 4 + (n * H + fo) % 4).then_inc(pe_z, 1)
                if late is None:
                    pe.wait_ge(late_ready, 1)
                    late = pe.value_load(late_i[0:1, 0:1], min_val=0, max_val=E + NB)
                pe.wait_ge(acc_done, (l + 1) * ACC)
                with pe.If(late > 0):
                    for g in range(XGROUP):
                        pe.wait_ge(x_s, l * XGROUP + g + 1)
                        pe.wait_ge(x_got, 16 * (l * CROSS + (g + 1) * GROUP))
                        if g:
                            pe.wait_ge(x_acc, l * CROSS + g * GROUP)
                        for k in range(GROUP):
                            u = g * GROUP + k
                            for h in range(H):
                                mm = nc.tensor.matmul(bank[k // 2][:, (k % 2) * 256 + h * P:(k % 2) * 256 + (h + 1) * P],
                                                      msgs[:, u % BODY, h * P:(h + 1) * P], S[:, k, :], start=True, stop=True)
                        mm.then_inc(x_p, 1)
                    pe.wait_ge(x_acc, (l + 1) * CROSS)
                    pe.wait_ge(z_out, l * NB * H + len(EARLY) * H)
                    for n in range(len(EARLY) * H):
                        if n:
                            pe.wait_ge(x_zout, l * len(EARLY) * H + n)
                        z_block(n // H, n % H, 4).then_inc(x_z, 1)
                    pe.wait_ge(x_zout, (l + 1) * len(EARLY) * H)
                for n in range(len(EARLY) * H, NB * H):
                    if n >= 4:
                        pe.wait_ge(z_out, l * NB * H + n - 3)
                    z_block(n // H, n % H, 4 + n % 4).then_inc(pe_z, 1)
                pe.wait_ge(z_out, (l + 1) * NB * H)
            for j, (t, w) in enumerate(PAIRS):
                need = min(NB, -(-(t + w) * P // 512))
                pe.wait_ge(act_in, (NB + need) * H)
                if j >= 2:
                    pe.wait_ge(x1_ready, j - 1)
                for k in range(w):
                    for h in range(H):
                        mm = nc.tensor.transpose(bank[j % 2][:, k * D + h * P:k * D + (h + 1) * P],
                                                 zT[:, h, (t + k) * P:(t + k + 1) * P], ident[:, :])
                mm.then_inc(pe_back, 1)
            for j in range(NP + 2):
                if j < NP:
                    rows_to_T(1, j)
                if j < 2:
                    continue
                j -= 2
                t, w = PAIRS[j]
                pe.wait_ge(tr_out, NP + j + 1)
                for k in range(w):
                    o = bank[2][:, (t + k) * NE:(t + k + 1) * NE]
                    for h in range(H):
                        nc.tensor.matmul(o, aggT[:, h, (t + k) * P:(t + k + 1) * P], gw[:, h, :], start=(h == 0), stop=False)
                    mm = nc.tensor.matmul(o, ones[0:1, :], gb[:, :], start=False, stop=True)
            mm.then_inc(pe_gate, 1)
            pe.wait_ge(hot_ready, 1)
            hots = hot[:, :, :].rearrange("p t e -> p (t e)")
            nc.tensor.matmul(bank[3][:, 0:TILES * NE], upper[:, :], hots, start=True, stop=True)
            nc.tensor.matmul(bank[4][:, 0:TILES * NE], ones[:, :], hots, start=True, stop=True).then_inc(pe_rank, 1)

            def expert_in(e):
                pe.wait_ge(erow_in[e % 2], 16 * (e // 2 + 1))
                for h in range(H):
                    for s in range(ST):
                        mm = nc.tensor.transpose(bank[h][:, s * P:(s + 1) * P], erow[e % 2][:, s, h * P:(h + 1) * P], ident[:, :])
                mm.then_inc(pe_in, 1)

            expert_in(0)
            for e in range(NE):
                pe.wait_ge(in_out, e + 1)
                pe.wait_ge(w_in[e % 2], 48 * (e // 2 + 1))
                for f in range(FT):
                    n = e * FT + f
                    if n >= 3:
                        pe.wait_ge(hid_out, n - 2)
                    for h in range(H):
                        mm = nc.tensor.matmul(bank[2 + n % 3][:, 0:CAP], we1[:, e % 2, h, f * P:(f + 1) * P], inT[e % 2][:, h, 0:CAP],
                                              start=(h == 0), stop=(h == H - 1))
                    mm.then_inc(pe_hid, 1)
                if e + 1 < NE:
                    expert_in(e + 1)
                pe.wait_ge(hid_out, (e + 1) * FT)
                for s in range(ST):
                    n = e * ST + s
                    if n >= 3:
                        pe.wait_ge(y_read, n - 2)
                    o = bank[5 + n % 3][:, 0:D]
                    for f in range(FT):
                        nc.tensor.matmul(o, hid[e % 2][:, f, s * P:(s + 1) * P], we2[:, e % 2, f, :], start=(f == 0), stop=False)
                    nc.tensor.matmul(o, ones[0:1, :], be2[:, e % 2, :], start=False, stop=True).then_inc(pe_y, 1)

        @block.scalar
        def _(act):
            def layernorm_sqrt(n, g):
                a, b = XG[g]
                act.wait_ge(var_ready, n * len(XG) + g + 1)
                nc.scalar.activation(sq[:, a:b], sd[:, a:b], ACT.Sqrt).then_inc(sqrt_done, 1)

            def T_out(n, to, j):
                t, w = PAIRS[j]
                act.wait_ge(pe_tr, n * NP + j + 1)
                nc.scalar.copy(to[:, :, t * P:(t + w) * P],
                               bank[6 + j % 2][:, :].rearrange("p (h n) -> p h n", h=H)[:, :, 0:w * P]).then_inc(tr_out, 1)

            def h_rows_out(l, j):
                t, w = PAIRS[j]
                act.wait_ge(pe_h, l * NP + j + 1)
                nc.scalar.activation(rows[:, t:t + w, 0:D], bank[4 + j % 2][:, 0:w * D].rearrange("p (t d) -> p t d", t=w),
                                     ACT.Relu).then_inc(h_out, 1)

            def z_out_block(j, fo, b):
                return nc.scalar.activation(zT[:, fo, 512 * j:512 * j + WIDTH[j]], bank[b][:, 0:WIDTH[j]], ACT.Identity,
                                            bias=vec(l, B2, fo))

            def norm_pairs(n, each):
                layernorm_sqrt(n, 0)
                for g in range(len(XG)):
                    if g + 1 < len(XG):
                        layernorm_sqrt(n, g + 1)
                    for j in range(XG[g][0] // 2, -(-XG[g][1] // 2)):
                        each(j)

            def stage(b, c0):
                nc.scalar.copy(idx_now[:, b, :], metaE[:, 0, bass.ds(c0, BLOCK)])
                nc.scalar.copy(relw_now[:, b, :, :], metaE[:, 1:3, bass.ds(c0, BLOCK)]).then_inc(staged, 1)

            act.wait_ge(meta_zero, 4)
            for l in range(2):
                for k in range(2):
                    act.dma_start(wc[:, l, k], conv[l]["w1" if k == 0 else "w2"].rearrange("(h p) n -> p h n", p=P)).then_inc(small_in, 16)
                act.dma_start(b1row[:, l, :], conv[l]["b1"].rearrange("(a n) -> a n", a=1)).then_inc(small_in, 16)
                for k, name in enumerate(("b2", "g", "b", "bng", "bnb")):
                    r = VEC + (l * 5 + k) * H
                    act.dma_start(colsrc[r:r + H, :], conv[l][name].rearrange("(h p) -> h p", p=P)).then_inc(small_in, 16)
            act.dma_start(colsrc[0:NE * FT, :], b1.rearrange("e (f p) -> (e f) p", p=P)).then_inc(small_in, 16)
            act.dma_start(gw[:, :, :], gate_w.rearrange("(h p) n -> p h n", p=P)).then_inc(small_in, 16)
            act.dma_start(gb[:, :], gate_b.rearrange("(a n) -> a n", a=1)).then_inc(small_in, 16)
            act.wait_ge(meta_in, 16 * 9)
            nc.scalar.copy(metaF[:, 0:2], metaI[:, :]).then_inc(meta_f, 1)

            def first_pair(j):
                if j == 0:
                    act.wait_ge(pe_meta, 1)
                    act.wait_ge(pads, 2)
                    for k in range(3):
                        nc.scalar.copy(metaE[:, k, 0:CHUNKS], bank[k][:, 0:CHUNKS]).then_inc(metaE_done, 1)
                    nc.scalar.copy(cols[:, :], bank[5][:, 0:P]).then_inc(metaE_done, 1)
                T_out(0, xnT, j)
                if j >= 2:
                    h_rows_out(0, j - 2)

            norm_pairs(0, first_pair)
            h_rows_out(0, NP - 2)
            h_rows_out(0, NP - 1)
            late = None
            for l in range(2):
                if l:
                    for j in range(NP):
                        h_rows_out(1, j)
                act.wait_ge(metaE_done, 5)
                stage(0, 0)
                stage(1, BLOCK)
                ends = [e + 1 for e in EARLY]
                for n, (a, b) in enumerate(zip([0] + ends, ends + [ITER - 1])):
                    with act.Fori(a, b, 1) as i:
                        for k in range(2):
                            act.wait_ge(acc_done, i * BODY + (l * ACC + GROUP + (k + 1) * BLOCK))
                            stage(k, i * BODY + (k + 2) * BLOCK)
                    if n < len(EARLY):
                        if n == 0 and l == 0:
                            act.wait_ge(filled, 16 * NE * ST)
                        for fo in range(H):
                            act.wait_ge(pe_z, l * NB * H + n * H + fo + 1)
                            z_out_block(n, fo, 4 + (n * H + fo) % 4).then_inc(z_out, 1)
                act.wait_ge(acc_done, l * ACC + GROUP + (BLOCKS - 1) * BLOCK)
                stage(0, CHUNKS)
                if late is None:
                    act.wait_ge(late_ready, 1)
                    late = act.value_load(late_i[0:1, 0:1], min_val=0, max_val=E + NB)
                with act.If(late > 0):
                    for n in range(len(EARLY) * H):
                        act.wait_ge(x_z, l * len(EARLY) * H + n + 1)
                        z_out_block(n // H, n % H, 4).then_inc(x_zout, 1)
                for n in range(len(EARLY) * H, NB * H):
                    act.wait_ge(pe_z, l * NB * H + n + 1)
                    z_out_block(n // H, n % H, 4 + n % 4).then_inc(z_out, 1)
                for k in range(2):
                    act.wait_ge(bvar_ready, 2 * l + k + 1)
                    nc.scalar.activation(bsq[:, :], bsd[:, :], ACT.Sqrt).then_inc(bsqrt_done, 1)
                    act.wait_ge(coef_ready, 2 * l + k + 1)
                    for n in range(NB * H):
                        j, fo = divmod(n, H)
                        a = zT[:, fo, 512 * j:512 * j + WIDTH[j]]
                        if k == 0:
                            nc.scalar.activation(a, a, ACT.Relu, bias=bof[:, fo:fo + 1], scale=bsc[:, fo:fo + 1]).then_inc(y_out, 1)
                        elif l == 0:
                            nc.scalar.activation(a, a, ACT.Relu, bias=bof[:, fo:fo + 1], scale=bsc[:, fo:fo + 1]).then_inc(act_in, 1)
                        else:
                            act.wait_ge(res_mul, n + 1)
                            nc.scalar.activation(a, a, ACT.Relu, bias=bof[:, fo:fo + 1]).then_inc(act_in, 1)
            norm_pairs(1, lambda j: T_out(1, aggT, j))
            act.wait_ge(lg_ready, 1)
            nc.scalar.activation(ex[:, :, :], lg[:, :, :], ACT.Exp).then_inc(exp_done, 1)
            for e in range(NE):
                act.wait_ge(pe_in, e + 1)
                if e >= 2:
                    act.wait_ge(pe_y, ST * (e - 1))
                for h in range(H):
                    c = nc.scalar.copy(inT[e % 2][:, h, :], bank[h][:, :])
                c.then_inc(in_out, 1)
                for f in range(FT):
                    n = e * FT + f
                    act.wait_ge(pe_hid, n + 1)
                    nc.scalar.activation(hid[e % 2][:, f, 0:CAP], bank[2 + n % 3][:, 0:CAP], ACT.Relu,
                                         bias=expert_bias(e, f)).then_inc(hid_out, 1)

        @block.vector
        def _(dve):
            chain = [0]

            def then(ins):
                chain[0] += 1
                ins.then_inc(dve_chain, 1)
                dve.wait_ge(dve_chain, chain[0])

            def layernorm(n, arrived, between=lambda: None):
                def normed(g):
                    a, b = XG[g]
                    dve.wait_ge(sqrt_done, n * len(XG) + g + 1)
                    then(nc.vector.reciprocal(rs[:, a:b], sq[:, a:b]))
                    for t in range(a, b):
                        nc.vector.tensor_scalar(rows[:, t, 0:D], rows[:, t, D:2 * D], mv[:, t, 0:1], rs[:, t:t + 1],
                                                ALU.subtract, ALU.mult).then_inc(rows_norm, 1)

                for g, (a, b) in enumerate(XG):
                    for t in range(a, b):
                        arrived(t)
                        c = nc.vector.bn_stats(st[:, t, :], rows[:, t, D:2 * D])
                    then(c)
                    for t in range(a, b):
                        c = nc.vector.bn_aggr(mv[:, t, :], st[:, t, :])
                    then(c)
                    nc.vector.tensor_scalar(sd[:, a:b], mv[:, a:b, 1], EPS, None, ALU.add).then_inc(var_ready, 1)
                    if g == 0:
                        between()
                    else:
                        normed(g - 1)
                normed(len(XG) - 1)

            nc.vector.memset(rows[:, TILES - 1, D:2 * D], 0.0).then_inc(tail_zero, 1)

            def edges_prepared():
                dve.wait_ge(consts, 10)
                nc.vector.tensor_copy(iota_f[:, :], iota_i[:, :])
                nc.vector.tensor_copy(rank[:, :], rank_i[:, :])
                nc.vector.tensor_copy(base[:, :], base_i[:, :])
                nc.vector.tensor_copy(tok_f[:, :], tok_i[:, :])
                nc.vector.tensor_copy(rows[:, :, 2 * D].bitcast(I32), tok_i[:, :])
                then(nc.vector.tensor_copy(bound[:, :], bound_i[:, :]))
                dve.wait_ge(meta_f, 1)
                for g in range(GROUPS):
                    nc.vector.tensor_scalar(gt_first[:, g, :], bound[:, :], metaF[:, 1, g, 0:1], None, ALU.is_gt)
                    c = nc.vector.tensor_scalar(relT[:, g, :], metaF[:, 1, g, :], metaF[:, 1, g, 0:1], None, ALU.subtract)
                then(c)
                for g in range(GROUPS):
                    nc.vector.scalar_tensor_tensor(out=pick[:, g, :], in0=bound[:, :], scalar=metaF[:, 1, g, P - 1:P],
                                                   in1=gt_first[:, g, :], op0=ALU.is_le, op1=ALU.mult)
                nc.vector.tensor_scalar(farW, metaF[:, 2], 0.0, None, ALU.not_equal)
                then(nc.vector.tensor_scalar(far, relT, float(P), None, ALU.is_ge))
                then(nc.vector.tensor_tensor(farW, farW, far, ALU.mult))
                then(nc.vector.tensor_reduce(nfar[:, :], farW, AX_X, ALU.add))
                nc.vector.tensor_tensor(farW, metaF[:, 2], far, ALU.mult).then_inc(meta_rel, 1)

            def x_arrived(t):
                g = next(g for g, (a, b) in enumerate(XG) if a <= t < b)
                if XG[g][0] == t:
                    dve.wait_ge(x_in[g], 32 if XG[g][1] == TILES else 16)

            layernorm(0, x_arrived, edges_prepared)
            dve.wait_ge(pe_meta, 1)
            dve.wait_ge(metaE_done, 4)
            nc.vector.tensor_copy(idx_x[:, :], bank[3][:, 0:CROSS])
            nc.vector.tensor_tensor(metaX[:, 1, :], bank[3][:, 32:32 + CROSS], bound[:, :], ALU.subtract)
            nc.vector.tensor_copy(metaX[:, 2, :], bank[3][:, 64:64 + CROSS])
            nc.vector.tensor_copy(late_f[:, NB:], bank[3][0:1, 24:25])
            nc.vector.tensor_copy(offs[:, :], bank[3][0:1, 96:96 + CHUNKS])
            nc.vector.tensor_copy(offs_f[:, :], bank[3][0:1, 96:96 + CHUNKS]).then_inc(metaE_done, 1)
            dve.wait_ge(metaE_done, 5)
            nc.vector.memset(late_f[:, len(EARLY):NB], 0.0)
            for j, i in enumerate(EARLY):
                c = nc.vector.tensor_scalar(late_f[:, j:j + 1], offs_f[:, i * BODY:i * BODY + 1], 512.0 * (j + 1), None, ALU.is_lt)
            then(c)
            then(nc.vector.tensor_reduce(late_f[:, 0:1], late_f[:, :], AX_X, ALU.add))
            nc.vector.tensor_copy(late_i[:, :], late_f[:, 0:1]).then_inc(late_ready, 1)
            dve.wait_ge(late_ready, 1)
            late = dve.value_load(late_i[0:1, 0:1], min_val=0, max_val=E + NB)

            def build_S(half, q):
                b, c0 = (q // 2) % 2, (q % 2) * GROUP
                for k in range(GROUP):
                    c = nc.vector.tensor_scalar(S[:, half * GROUP + k, :], iota_f[:, :], relw_now[:, b, 0, c0 + k:c0 + k + 1],
                                                relw_now[:, b, 1, c0 + k:c0 + k + 1], ALU.is_equal, ALU.mult)
                c.then_inc(s_ready, 1)

            def stats(j, fo):
                return nc.vector.bn_stats(bst[:, fo, j, :], zT[:, fo, 512 * j:512 * j + WIDTH[j]])

            for l in range(2):
                if l:
                    dve.wait_ge(pe_z, l * NB * H)
                nc.vector.memset(aggT[:, :, :], 0.0).then_inc(acc_done, GROUP)
                dve.wait_ge(staged, l * (BLOCKS + 1) + 1)
                build_S(0, 0)
                ends = [e + 2 for e in EARLY]
                for n, (a, b) in enumerate(zip([0] + ends, ends + [ITER])):
                    with dve.Fori(a, b, 1) as i:
                        for q in range(4):
                            dve.wait_ge(p_ready, i * 4 + (l * NGROUP + q))
                            if q % 2:
                                dve.wait_ge(staged, i * 2 + (l * (BLOCKS + 1) + (q + 1) // 2 + 1))
                            build_S((q + 1) % 2, q + 1)
                            _, at = nc.values_load_multi_w_load_instructions(
                                offs[0:1, bass.ds(i * BODY + q * GROUP, GROUP)], engines=[mybir.EngineType.DVE],
                                min_val=0, max_val=N - 1, skip_runtime_bounds_check_because="dst lies in [0, N)")
                            dve.wait_ge(p_ready, i * 4 + (l * NGROUP + q + 1))
                            for k in range(GROUP):
                                dve.wait_ge(acc_done, i * BODY + (l * ACC + GROUP + q * GROUP + k))
                                a = aggT[:, :, bass.ds(at[k], P)]
                                o = bank[2 * (q % 2) + k // 2][:, (k % 2) * 256:(k % 2 + 1) * 256].rearrange("p (h n) -> p h n", h=H)
                                nc.vector.tensor_tensor(a, a, o, ALU.add).then_inc(acc_done, 1)
                    if n < len(EARLY):
                        for fo in range(H):
                            dve.wait_ge(z_out, l * NB * H + n * H + fo + 1)
                            stats(n, fo)
                with dve.If(late > 0):
                    dve.wait_ge(acc_done, (l + 1) * ACC)
                    for g in range(XGROUP):
                        if g:
                            dve.wait_ge(x_p, l * XGROUP + g)
                        for k in range(GROUP):
                            u = g * GROUP + k
                            c = nc.vector.tensor_scalar(S[:, k, :], iota_f[:, :], metaX[:, 1, u:u + 1], metaX[:, 2, u:u + 1],
                                                        ALU.is_equal, ALU.mult)
                        c.then_inc(x_s, 1)
                        dve.wait_ge(x_p, l * XGROUP + g + 1)
                        for k in range(GROUP):
                            u = g * GROUP + k
                            a = aggT[:, :, (u + 1) * P:(u + 2) * P]
                            o = bank[k // 2][:, (k % 2) * 256:(k % 2 + 1) * 256].rearrange("p (h n) -> p h n", h=H)
                            nc.vector.tensor_tensor(a, a, o, ALU.add).then_inc(x_acc, 1)
                    for n in range(len(EARLY) * H):
                        dve.wait_ge(x_zout, l * len(EARLY) * H + n + 1)
                        stats(n // H, n % H)

                for k in range(2):
                    for n in range(0 if k else len(EARLY) * H, NB * H):
                        dve.wait_ge(y_out if k else z_out, l * NB * H + n + 1)
                        c = stats(n // H, n % H)
                    then(c)
                    for fo in range(H):
                        c = nc.vector.bn_aggr(bmv[:, fo, :], bst[:, fo, :, :].rearrange("p j s -> p (j s)"))
                    then(c)
                    nc.vector.tensor_scalar(bsd[:, :], bmv[:, :, 1], EPS, None, ALU.add).then_inc(bvar_ready, 1)
                    dve.wait_ge(bsqrt_done, 2 * l + k + 1)
                    then(nc.vector.reciprocal(brs[:, :], bsq[:, :]))
                    then(nc.vector.tensor_tensor(bsc[:, :], brs[:, :], vec(l, (G, BNG)[k]), ALU.mult))
                    then(nc.vector.tensor_tensor(bms[:, :], bmv[:, :, 0], bsc[:, :], ALU.mult))
                    nc.vector.tensor_tensor(bof[:, :], vec(l, (B, BNB)[k]), bms[:, :], ALU.subtract).then_inc(coef_ready, 1)
            dve.wait_ge(coef_ready, 4)
            for n in range(NB * H):
                j, fo = divmod(n, H)
                a = zT[:, fo, 512 * j:512 * j + WIDTH[j]]
                nc.vector.scalar_tensor_tensor(out=a, in0=a, scalar=bsc[:, fo:fo + 1], in1=xnT[:, fo, 512 * j:512 * j + WIDTH[j]],
                                               op0=ALU.mult, op1=ALU.add).then_inc(res_mul, 1)
            for j, (t, w) in enumerate(PAIRS):
                dve.wait_ge(pe_back, j + 1)
                nc.vector.tensor_tensor(rows[:, t:t + w, D:2 * D], rows[:, t:t + w, D:2 * D],
                                        bank[j % 2][:, 0:w * D].rearrange("p (t d) -> p t d", t=w), ALU.add).then_inc(x1_ready, 1)
            dve.wait_ge(h_stored, 16 * 10)
            layernorm(1, lambda t: dve.wait_ge(x1_ready, t // 2 + 1))
            dve.wait_ge(pe_gate, 1)
            L = bank[2][:, 0:TILES * NE].rearrange("p (t e) -> p t e", e=NE)

            def wide(a):
                return a[:, :].rearrange("p (t o) -> p t o", o=1).broadcast_to([P, TILES, NE])

            def each(a):
                return a[:, :].rearrange("p (o e) -> p o e", o=1).broadcast_to([P, TILES, NE])

            then(nc.vector.tensor_reduce(r1[:, :], L, AX_X, ALU.max))
            nc.vector.tensor_tensor(lg[:, :, :], L, wide(r1), ALU.subtract).then_inc(lg_ready, 1)
            dve.wait_ge(exp_done, 1)
            nc.vector.tensor_reduce(r1[:, :], ex[:, :, :], AX_X, ALU.max)
            then(nc.vector.tensor_reduce(r2[:, :], ex[:, :, :], AX_X, ALU.add))
            then(nc.vector.reciprocal(r3[:, :], r2[:, :]))
            nc.vector.tensor_tensor(rows[:, :, 2 * D + 1], r1[:, :], r3[:, :], ALU.mult)
            then(nc.vector.tensor_tensor(hot[:, :, :], ex[:, :, :], wide(r1), ALU.is_equal))
            then(nc.vector.tensor_tensor(hot[:, :, :], hot[:, :, :], each(rank), ALU.mult))
            then(nc.vector.tensor_reduce(r2[:, :], hot[:, :, :], AX_X, ALU.max))
            then(nc.vector.tensor_tensor(hot[:, :, :], hot[:, :, :], wide(r2), ALU.is_equal))
            then(nc.vector.tensor_scalar(r3[:, :], tok_f[:, :], float(N), None, ALU.is_lt))
            nc.vector.tensor_tensor(hot[:, :, :], hot[:, :, :], wide(r3), ALU.mult).then_inc(hot_ready, 1)
            dve.wait_ge(pe_rank, 1)
            then(nc.vector.tensor_copy(tot[:, :, :].rearrange("p t e -> p (t e)"), bank[4][:, 0:TILES * NE]))
            nc.vector.memset(cum[:, 0, :], 0.0)
            then(nc.vector.tensor_copy(cum[:, 1, :], tot[:, 0, :]))
            for t in range(2, TILES):
                then(nc.vector.tensor_tensor(cum[:, t, :], cum[:, t - 1, :], tot[:, t - 1, :], ALU.add))
            then(nc.vector.tensor_tensor(cum[:, :, :], cum[:, :, :], bank[3][:, 0:TILES * NE].rearrange("p (t e) -> p t e", e=NE), ALU.add))
            nc.vector.tensor_tensor(tot[:, :, :], hot[:, :, :], each(base), ALU.mult)
            then(nc.vector.tensor_tensor(cum[:, :, :], cum[:, :, :], hot[:, :, :], ALU.mult))
            nc.vector.tensor_reduce(r1[:, :], cum[:, :, :], AX_X, ALU.add)
            then(nc.vector.tensor_reduce(r2[:, :], tot[:, :, :], AX_X, ALU.add))
            nc.vector.tensor_scalar(r4[:, :], r1[:, :], float(CAP), float(FAR), ALU.is_gt, ALU.mult)
            then(nc.vector.scalar_tensor_tensor(out=r2[:, :], in0=r1[:, :], scalar=-1.0, in1=r2[:, :], op0=ALU.add, op1=ALU.add))
            nc.vector.tensor_scalar(r3[:, :], r3[:, :], -float(FAR), float(FAR), ALU.mult, ALU.add)
            then(nc.vector.tensor_tensor(r2[:, :], r2[:, :], r4[:, :], ALU.add))
            nc.vector.tensor_tensor(slot_i[:, :], r2[:, :], r3[:, :], ALU.add).then_inc(slots_ready, 1)

            for i in range(NE * ST):
                e, s = divmod(i, ST)
                er = erow[e % 2]
                dve.wait_ge(pe_y, i + 1)
                nc.vector.tensor_scalar(yv, bank[5 + i % 3][:, 0:D], er[:, s, 2 * D + 1:2 * D + 2], None, ALU.mult).then_inc(y_read, 1)
                dve.wait_ge(y_read, i + 1)
                nc.vector.tensor_tensor(ymask, yv, yv, ALU.subtract)
                nc.vector.tensor_scalar(ya, yv, FLT_MAX, NAN_TO_NUM_INF, ALU.is_gt, ALU.mult)
                if i >= 4:
                    dve.wait_ge(y_sent[i % 4], 16 * (i // 4))
                then(nc.vector.tensor_scalar(yo[:, i % 4, :], yv, -FLT_MAX, -NAN_TO_NUM_INF, ALU.is_lt, ALU.mult))
                then(nc.vector.tensor_tensor(ya, ya, yo[:, i % 4, :], ALU.add))
                then(nc.vector.copy_predicated(yv, ymask.bitcast(U32), ya))
                nc.vector.tensor_tensor(yo[:, i % 4, :], yv, er[:, s, D:2 * D], ALU.add).then_inc(y_ready, 1)
                dve.wait_ge(y_ready, i + 1)


_INS = ["x", "src", "dst", "edge_weight"] + [f"L0_gnn_{k}" for k in (
    "c1_w1", "c1_b1", "c1_w2", "c1_b2", "c1_g", "c1_b", "bn1_g", "bn1_b",
    "c2_w1", "c2_b1", "c2_w2", "c2_b2", "c2_g", "c2_b", "bn2_g", "bn2_b")] + [
    f"L0_ffn_{k}" for k in ("gate_w", "gate_b", "w1", "b1", "w2", "b2")]


def build(nc, ap, out):
    conv = []
    for l in (1, 2):
        c = {k: ap[f"L0_gnn_c{l}_{k}"] for k in ("w1", "b1", "w2", "b2", "g", "b")}
        c["bng"], c["bnb"] = ap[f"L0_gnn_bn{l}_g"], ap[f"L0_gnn_bn{l}_b"]
        conv.append(c)
    f = {k: ap[f"L0_ffn_{k}"] for k in ("gate_w", "gate_b", "w1", "b1", "w2", "b2")}
    gnn_moe_program(nc, ap["x"], ap["src"], ap["dst"], ap["edge_weight"], conv, f["gate_w"], f["gate_b"],
                    f["w1"], f["b1"], f["w2"], f["b2"], out)


def kernel(**inputs):
    import numpy as _np
    import concourse.bacc as _bacc
    from concourse.bass_utils import run_bass_kernel_spmd as _run

    nc = _bacc.Bacc("TRN2", target_bir_lowering=False, num_devices=1)
    arrays, aps = {}, {}
    for name in _INS:
        a = _np.ascontiguousarray(inputs[name])
        arrays[f"in_{name}"] = a
        aps[name] = nc.dram_tensor(f"in_{name}", a.shape, mybir.dt.from_np(a.dtype), kind="ExternalInput").ap()
    out = nc.dram_tensor("out_x", arrays["in_x"].shape, F32, kind="ExternalOutput").ap()
    build(nc, aps, out)
    r = _run(nc, [arrays], core_ids=[0])
    return r.results[0]["out_x"]
```

```python
from contextlib import ExitStack

import numpy as np

import concourse.bass as bass
from concourse import mybir

F32 = mybir.dt.float32
I32 = mybir.dt.int32
U32 = mybir.dt.uint32
ALU = mybir.AluOpType
ACT = mybir.ActivationFunctionType
AX_X = mybir.AxisListType.X

P = 128
EPS = 1e-5
FLT_MAX = float(np.finfo(np.float32).max)
NAN_TO_NUM_INF = 1e4


def gnn_moe_program(nc, x, src, dst, ew, conv, gate_w, gate_b, w1, b1, w2, b2, out):
    N, D = x.shape
    (E,) = src.shape
    NE, _, F = w1.shape
    H = D // P
    TILES = -(-N // P)
    TAIL = N - (TILES - 1) * P
    NPAD = TILES * P
    CHUNKS = -(-E // P)
    GROUPS = -(-CHUNKS // P)
    CROSS = TILES - 1
    BLOCK = 8
    GROUP = 4
    BODY = 2 * BLOCK
    ITER = CHUNKS // BODY
    BLOCKS = CHUNKS // BLOCK
    NGROUP = CHUNKS // GROUP
    XGROUP = CROSS // GROUP
    assert CROSS <= 24 and 96 + CHUNKS <= 512
    assert CHUNKS % BODY == 0 and CROSS % GROUP == 0 and H == 2
    NB = -(-N // 512)
    EARLY = [-(-(CHUNKS * 512 * (j + 1) // N + 8 + GROUP) // BODY) for j in range(NB)]
    EARLY = [i for i in EARLY if i <= ITER - 3]
    FT = F // P
    CAP = max(1, -(-5 * N // (4 * NE)))
    ESLOT = 512
    ST = ESLOT // P
    ROW = 2 * D + 2
    FAR = 1 << 20
    assert CAP <= ESLOT
    XG = [(0, 4), (4, 10), (10, 16), (16, 22), (22, TILES)]

    h_dram = [nc.dram_tensor(f"h{l}", (N, D), F32, kind="Internal").ap() for l in range(2)]
    ebuf = nc.dram_tensor("expert_rows", (NE * ESLOT, ROW), F32, kind="Internal").ap()

    with ExitStack() as ctx:
        def sb(name, shape, dt=F32):
            return ctx.enter_context(nc.sbuf_tensor(name, shape, dt))

        def sem(name):
            return ctx.enter_context(nc.semaphore(name))

        rows = sb("rows", [P, TILES, ROW])
        xnT = sb("xnT", [P, H, NPAD])
        aggT = sb("aggT", [P, H, NPAD + P])
        zT = sb("zT", [P, H, NPAD])
        msgs = sb("msgs", [P, BODY, D])
        S = sb("S", [P, 2 * GROUP, P])
        edges = aggT[:, :, :].rearrange("p h n -> p (h n)")
        GE = GROUPS * P
        metaI = edges[:, 0:2 * GE].bitcast(I32).rearrange("p (k g e) -> p k g e", k=2, e=P)
        metaF = edges[:, 2 * GE:5 * GE].rearrange("p (k g e) -> p k g e", k=3, e=P)
        relT = edges[:, 5 * GE:6 * GE].rearrange("p (g e) -> p g e", e=P)
        metaE = sb("metaE", [P, 3, CHUNKS + BLOCK])
        metaX = sb("metaX", [P, 3, CROSS])
        idx_x = sb("idx_x", [P, CROSS], I32)
        idx_now = sb("idx_now", [P, 2, BLOCK], I32)
        relw_now = sb("relw_now", [P, 2, 2, BLOCK])
        offs_f = sb("offs_f", [1, CHUNKS])
        offs = sb("offs", [1, CHUNKS], I32)
        late_f = sb("late_f", [1, NB + 1])
        late_i = sb("late_i", [1, 1], I32)
        iota_i = sb("iota_i", [P, P], I32)
        iota_f = sb("iota_f", [P, P])
        bound_i = sb("bound_i", [P, CROSS], I32)
        bound = sb("bound", [P, CROSS])
        gt_first, pick = (
            edges[:, 6 * GE + P + k * GROUPS * CROSS:6 * GE + P + (k + 1) * GROUPS * CROSS].rearrange("p (g u) -> p g u", g=GROUPS)
            for k in range(2))
        nfar = sb("nfar", [P, GROUPS])
        ident = sb("ident", [P, P])
        upper = sb("upper", [P, P])
        ones = sb("ones", [P, P])
        wc = sb("wc", [P, 2, 2, H, D])
        b1row = sb("b1row", [P, 2, D])
        colsrc = S[:, 2 * GROUP - 1, :]
        farW = edges[:, 7 * GE:8 * GE].rearrange("p (g e) -> p g e", e=P)
        far = edges[:, 8 * GE:9 * GE].rearrange("p (g e) -> p g e", e=P)
        cols = sb("cols", [P, P])
        gw = sb("gw", [P, H, NE])
        gb = sb("gb", [P, NE])
        we1 = sb("we1", [P, 2, H, F])
        we2 = sb("we2", [P, 2, FT, D])
        be2 = sb("be2", [P, 2, D])
        st = sb("st", [P, TILES, 6])
        mv = sb("mv", [P, TILES, 2])
        sd = sb("sd", [P, TILES])
        sq = sb("sq", [P, TILES])
        rs = sb("rs", [P, TILES])
        warm = sb("warm", [P, 1])
        nmr = sb("nmr", [P, TILES])
        bst = sb("bst", [P, H, NB, 6])
        bmv = sb("bmv", [P, H, 2])
        bsd = sb("bsd", [P, H])
        bsq = sb("bsq", [P, H])
        brs = sb("brs", [P, H])
        bsc = sb("bsc", [P, H])
        bms = sb("bms", [P, H])
        bof = sb("bof", [P, H])
        lg, ex, hot, tot, cum = (
            xnT[:, 1, NPAD - (k + 1) * TILES * NE:NPAD - k * TILES * NE].rearrange("p (t e) -> p t e", e=NE) for k in range(5))
        rank_i = sb("rank_i", [P, NE], I32)
        rank = sb("rank", [P, NE])
        base_i = sb("base_i", [P, NE], I32)
        base = sb("base", [P, NE])
        r1 = sb("r1", [P, TILES])
        r2 = sb("r2", [P, TILES])
        r3 = sb("r3", [P, TILES])
        r4 = sb("r4", [P, TILES])
        tok_i = sb("tok_i", [P, TILES], I32)
        tok_f = sb("tok_f", [P, TILES])
        slot_i = sb("slot_i", [P, TILES], I32)

        xf, zf, af = (t[:, :, :].rearrange("p h n -> p (h n)") for t in (xnT, zT, aggT))
        hid = [b[:, 0:FT * ESLOT].rearrange("p (f s) -> p f s", f=FT) for b in (xf, zf)]
        inT = [b[:, FT * ESLOT:(FT + H) * ESLOT].rearrange("p (h s) -> p h s", h=H) for b in (xf, zf)]
        erow = [af[:, i * ST * ROW:(i + 1) * ST * ROW].rearrange("p (s r) -> p s r", s=ST) for i in range(2)]
        yv = af[:, 2 * ST * ROW:2 * ST * ROW + D]
        ymask = af[:, 2 * ST * ROW + D:2 * ST * ROW + 2 * D]
        ya = af[:, 2 * ST * ROW + 2 * D:2 * ST * ROW + 3 * D]
        yo = msgs[:, 0:4, :]
        fill = we1[:, 1, 0, 0:ROW]

        bank = [ctx.enter_context(nc.psum_tensor(f"bank{i}", [P, 512], F32)) for i in range(8)]

        x_in = [sem(f"x_in{g}") for g in range(len(XG))]
        meta_zero = sem("meta_zero")
        meta_in = sem("meta_in")
        w1_in = sem("w1_in")
        small_in = sem("small_in")
        consts = sem("consts")
        pads = sem("pads")
        tail_zero = sem("tail_zero")
        fill_ready = sem("fill_ready")
        filled = sem("filled")
        dve_chain = sem("dve_chain")
        meta_f = sem("meta_f")
        meta_rel = sem("meta_rel")
        pe_meta = sem("pe_meta")
        metaE_done = sem("metaE_done")
        cols_in = sem("cols_in")
        pe_cols = sem("pe_cols")
        cols_done = sem("cols_done")
        norm_coef = sem("norm_coef")
        h_sum = sem("h_sum")
        var_ready = sem("var_ready")
        sqrt_done = sem("sqrt_done")
        rows_norm = sem("rows_norm")
        pe_tr = sem("pe_tr")
        tr_out = sem("tr_out")
        pe_h = sem("pe_h")
        h_out = sem("h_out")
        h_stored = sem("h_stored")
        staged = sem("staged")
        pool_go = sem("pool_go")
        got = [sem(f"got{j}") for j in range(BODY)]
        s_ready = sem("s_ready")
        p_ready = sem("p_ready")
        late_ready = sem("late_ready")
        x_got = sem("x_got")
        x_s = sem("x_s")
        x_p = sem("x_p")
        x_acc = sem("x_acc")
        x_z = sem("x_z")
        x_zout = sem("x_zout")
        acc_done = sem("acc_done")
        pe_z = sem("pe_z")
        z_out = sem("z_out")
        bvar_ready = sem("bvar_ready")
        bsqrt_done = sem("bsqrt_done")
        coef_ready = sem("coef_ready")
        y_out = sem("y_out")
        act_in = sem("act_in")
        res_mul = sem("res_mul")
        pe_back = sem("pe_back")
        x1_ready = sem("x1_ready")
        pe_gate = sem("pe_gate")
        lg_ready = sem("lg_ready")
        exp_done = sem("exp_done")
        hot_ready = sem("hot_ready")
        pe_rank = sem("pe_rank")
        slots_ready = sem("slots_ready")
        x1_stored = sem("x1_stored")
        dispatched = sem("dispatched")
        w_in = [sem(f"w_in{i}") for i in range(2)]
        erow_in = [sem(f"erow_in{i}") for i in range(2)]
        pe_in = sem("pe_in")
        in_out = sem("in_out")
        pe_hid = sem("pe_hid")
        hid_out = sem("hid_out")
        pe_y = sem("pe_y")
        y_read = sem("y_read")
        y_ready = sem("y_ready")
        y_sent = [sem(f"y_sent{i}") for i in range(4)]

        def expert_bias(e, f):
            return cols[:, e * FT + f:e * FT + f + 1]

        B2, G, B, BNG, BNB = range(5)
        VEC = NE * FT

        def vec(l, which, h=None):
            c = VEC + (l * 5 + which) * H
            return cols[:, c:c + H] if h is None else cols[:, c + h:c + h + 1]

        PAIRS = [(2 * j, min(2, TILES - 2 * j)) for j in range(-(-TILES // 2))]
        NP = len(PAIRS)
        EDGES_AT = 3
        WIDTH = [min(512, N - 512 * j) for j in range(NB)]
        ZEROED = 2 * GROUP
        ACC = ZEROED + CHUNKS

        T_BANKS = ((6, 7), (5, 6, 7))
        H_BANKS = (4, 5, 0, 1)
        BACK_BANKS = (0, 1, 3, 4)
        STORES = len(XG) + 1
        xt = x[0:(TILES - 1) * P, :].rearrange("(t p) d -> p t d", p=P)

        block = ctx.enter_context(nc.Block())

        @block.sync
        def _(sp):
            def load_x(g):
                a, b = XG[g]
                if b == TILES:
                    sp.wait_ge(tail_zero, 1)
                    sp.dma_start(rows[0:TAIL, TILES - 1, D:2 * D], x[(TILES - 1) * P:, :]).then_inc(x_in[g], 16)
                    b -= 1
                sp.dma_start(rows[:, a:b, D:2 * D], xt[:, a:b, :]).then_inc(x_in[g], 16)

            load_x(1)
            whole, rest = CHUNKS - 1 - (GROUPS - 1) * P, E - (CHUNKS - 1) * P
            sp.wait_ge(meta_zero, 4)
            for ap, to in ((src, metaI[:, 0]), (dst, metaI[:, 1]), (ew, metaF[:, 2])):
                g3, cut = (GROUPS - 1) * P * P, (CHUNKS - 1) * P
                sp.dma_start(to[:, 0:GROUPS - 1, :], ap[0:g3].rearrange("(g c e) -> c g e", c=P, e=P)).then_inc(meta_in, 16)
                sp.dma_start(to[0:whole, GROUPS - 1, :], ap[g3:cut].rearrange("(c e) -> c e", e=P)).then_inc(meta_in, 16)
                sp.dma_start(to[whole:whole + 1, GROUPS - 1, 0:rest], ap[cut:E].rearrange("(c e) -> c e", c=1)).then_inc(meta_in, 16)
            for g in range(2, len(XG)):
                load_x(g)

            def load_expert(e):
                sp.dma_start(we1[:, e % 2], w1[e].rearrange("(h p) f -> p h f", p=P)).then_inc(w_in[e % 2], 16)
                sp.dma_start(we2[:, e % 2], w2[e].rearrange("(f p) n -> p f n", p=P)).then_inc(w_in[e % 2], 16)
                sp.dma_start(be2[:, e % 2, :], b2[e:e + 1, :].partition_broadcast(P)).then_inc(w_in[e % 2], 16)

            for l in range(2):
                ht = h_dram[l][0:(TILES - 1) * P, :].rearrange("(t p) d -> p t d", p=P)
                for a, b in XG:
                    sp.wait_ge(h_out, l * NP + -(-b // 2))
                    if b == TILES:
                        b -= 1
                        sp.dma_start(h_dram[l][b * P:, :], rows[0:TAIL, b, 0:D]).then_inc(h_stored, 16)
                    sp.dma_start(ht[:, a:b, :], rows[:, a:b, 0:D]).then_inc(h_stored, 16)
                if l == 0:
                    load_expert(0)
                    sp.wait_ge(fill_ready, 2)
                    with sp.Fori(0, NE * ST, 1) as i:
                        sp.wait_ge(acc_done, i * BLOCK + (ZEROED + BLOCK))
                        sp.dma_start(ebuf[bass.ds(i * P, P), :], fill).then_inc(filled, 16)
                    sp.wait_ge(filled, 16 * NE * ST)
                    load_expert(1)
            ot = out[0:(TILES - 1) * P, :].rearrange("(t p) d -> p t d", p=P)
            for a, b in XG:
                sp.wait_ge(x1_ready, -(-b // 2))
                if b == TILES:
                    b -= 1
                    sp.dma_start(out[b * P:, :], rows[0:TAIL, b, D:2 * D]).then_inc(x1_stored, 16)
                sp.dma_start(ot[:, a:b, :], rows[:, a:b, D:2 * D]).then_inc(x1_stored, 16)
            sp.wait_ge(dispatched, 16 * TILES)
            for e in range(NE):
                if e >= 2:
                    sp.wait_ge(y_ready, ST * (e - 1))
                    for i in range(4):
                        sp.wait_ge(y_sent[i], 16 * (e - 1))
                sp.dma_start(erow[e % 2], ebuf[e * ESLOT:(e + 1) * ESLOT, :].rearrange("(s p) r -> p s r", p=P)).then_inc(erow_in[e % 2], 16)
                if e >= 2:
                    load_expert(e)
            for i in range(4):
                sp.wait_ge(y_sent[i], 16 * (NE * ST // 4))

        @block.gpsimd
        def _(pool):
            nc.gpsimd.memset(metaI[:, 0, GROUPS - 1, :], 0).then_inc(meta_zero, 1)
            nc.gpsimd.memset(metaI[:, 1, GROUPS - 1, :], NPAD + P).then_inc(meta_zero, 1)
            nc.gpsimd.memset(metaF[:, 2, GROUPS - 1, :], 0.0).then_inc(meta_zero, 1)
            nc.gpsimd.memset(colsrc, 0.0).then_inc(meta_zero, 1)
            nc.gpsimd.iota(iota_i[:, :], [[1, P]], base=0, channel_multiplier=0).then_inc(consts, 1)
            nc.gpsimd.iota(bound_i[:, :], [[P, CROSS]], base=P, channel_multiplier=0).then_inc(consts, 1)
            nc.gpsimd.iota(rank_i[:, :], [[-1, NE]], base=NE, channel_multiplier=0).then_inc(consts, 1)
            nc.gpsimd.iota(base_i[:, :], [[ESLOT, NE]], base=0, channel_multiplier=0).then_inc(consts, 1)
            nc.gpsimd.iota(tok_i[:, :], [[P, TILES]], base=0, channel_multiplier=1).then_inc(consts, 1)
            nc.gpsimd.memset(ident[:, :], 0.0).then_inc(consts, 1)
            nc.gpsimd.memset(upper[:, :], 1.0).then_inc(consts, 1)
            nc.gpsimd.memset(ones[:, :], 1.0).then_inc(consts, 1)
            pool.wait_ge(consts, 8)
            nc.gpsimd.affine_select(out=ident[:, :], in_=ident[:, :], compare_op=ALU.not_equal, fill=1.0, base=0,
                                    pattern=[[-1, P]], channel_multiplier=1).then_inc(consts, 1)
            nc.gpsimd.affine_select(out=upper[:, :], in_=upper[:, :], compare_op=ALU.is_ge, fill=0.0, base=0,
                                    pattern=[[1, P]], channel_multiplier=-1).then_inc(consts, 1)
            nc.gpsimd.memset(fill, 0.0).then_inc(fill_ready, 1)
            pool.wait_ge(fill_ready, 1)
            nc.gpsimd.memset(fill[:, 2 * D:2 * D + 1].bitcast(I32), FAR).then_inc(fill_ready, 1)
            nc.gpsimd.memset(metaE[:, :, CHUNKS:], 0.0).then_inc(pads, 1)
            nc.gpsimd.memset(zT[:, :, N:], 0.0).then_inc(pads, 1)

            pool.wait_ge(meta_zero, 4)
            for l in range(2):
                for k in range(2):
                    if l or k:
                        pool.dma_start(wc[:, l, k], conv[l]["w1" if k == 0 else "w2"].rearrange("(h p) n -> p h n", p=P)).then_inc(small_in, 16)
                for k, name in enumerate(("b2", "g", "b", "bng", "bnb")):
                    r = VEC + (l * 5 + k) * H
                    pool.dma_start(colsrc[r:r + H, :], conv[l][name].rearrange("(h p) -> h p", p=P)).then_inc(cols_in, 16)
            pool.dma_start(b1row[:, 1, :], conv[1]["b1"].rearrange("(a n) -> a n", a=1).partition_broadcast(P)).then_inc(small_in, 16)
            pool.dma_start(colsrc[0:NE * FT, :], b1.rearrange("e (f p) -> (e f) p", p=P)).then_inc(cols_in, 16)
            pool.dma_start(gw[:, :, :], gate_w.rearrange("(h p) n -> p h n", p=P)).then_inc(small_in, 16)
            pool.dma_start(gb[:, :], gate_b.rearrange("(a n) -> a n", a=1).partition_broadcast(P)).then_inc(small_in, 16)

            late = None
            for l in range(2):
                if l == 0:
                    pool.wait_ge(pe_meta, 1)
                else:
                    pool.wait_ge(pe_z, NB * H)
                nc.gpsimd.memset(aggT[:, :, :], 0.0).then_inc(acc_done, ZEROED)
                pool.wait_ge(h_stored, 16 * STORES * (l + 1))
                with pool.Fori(0, ITER, 1) as i:
                    for b in range(2):
                        pool.wait_ge(staged, i * 2 + (l * (BLOCKS + 1) + b + 1))
                        pool.sem_inc(pool_go, 1)
                        for k in range(BLOCK):
                            nc.gpsimd.indirect_dma_start(
                                out=msgs[:, b * BLOCK + k, :], out_offset=None, in_=h_dram[l],
                                in_offset=bass.IndirectOffsetOnAxis(ap=idx_now[:, b, k:k + 1], axis=0),
                            ).then_inc(got[b * BLOCK + k], 16)
                if late is None:
                    pool.wait_ge(late_ready, 1)
                    late = pool.value_load(late_i[0:1, 0:1], min_val=0, max_val=E + NB)
                with pool.If(late > 0):
                    pool.wait_ge(acc_done, (l + 1) * ACC)
                    for u in range(CROSS):
                        if u >= BODY and u % GROUP == 0:
                            pool.wait_ge(x_acc, l * CROSS + u - BODY + GROUP)
                        nc.gpsimd.indirect_dma_start(
                            out=msgs[:, u % BODY, :], out_offset=None, in_=h_dram[l],
                            in_offset=bass.IndirectOffsetOnAxis(ap=idx_x[:, u:u + 1], axis=0),
                        ).then_inc(x_got, 16)
                        if u % GROUP == GROUP - 1:
                            pool.wait_ge(x_got, 16 * (l * CROSS + u + 1))
            pool.wait_ge(filled, 16 * NE * ST)
            pool.wait_ge(slots_ready, 1)
            for t in range(TILES):
                nc.gpsimd.indirect_dma_start(
                    out=ebuf, out_offset=bass.IndirectOffsetOnAxis(ap=slot_i[:, t:t + 1], axis=0),
                    in_=rows[:, t, :], in_offset=None, bounds_check=NE * ESLOT - 1, oob_is_err=False,
                ).then_inc(dispatched, 16)
            pool.wait_ge(x1_stored, 16 * STORES)
            for i in range(NE * ST):
                e, s = divmod(i, ST)
                pool.wait_ge(y_ready, i + 1)
                nc.gpsimd.indirect_dma_start(
                    out=out, out_offset=bass.IndirectOffsetOnAxis(ap=erow[e % 2][:, s, 2 * D:2 * D + 1].bitcast(I32), axis=0),
                    in_=yo[:, i % 4, :], in_offset=None, bounds_check=N - 1, oob_is_err=False,
                ).then_inc(y_sent[i % 4], 16)

        @block.tensor
        def _(pe):
            pe.wait_ge(consts, 10)

            def rows_to_T(n, j):
                t, w = PAIRS[j]
                pe.wait_ge(rows_norm, n * TILES + t + w)
                B = T_BANKS[n]
                if j >= len(B):
                    pe.wait_ge(tr_out, n * NP + j + 1 - len(B))
                for h in range(H):
                    for k in range(w):
                        mm = nc.tensor.transpose(bank[B[j % len(B)]][:, h * 256 + k * P:h * 256 + (k + 1) * P],
                                                 rows[:, t + k, h * P:(h + 1) * P], ident[:, :])
                mm.then_inc(pe_tr, 1)

            def h_rows(l, j):
                t, w = PAIRS[j]
                if l == 0:
                    pe.wait_ge(tr_out, j + 1)
                else:
                    pe.wait_ge(act_in, min(NB, -(-(t + w) * P // 512)) * H)
                if l == 0 and j == 2:
                    pe.wait_ge(metaE_done, 3)
                if j >= len(H_BANKS):
                    pe.wait_ge(h_sum, l * NP + j + 1 - len(H_BANKS))
                for k in range(w):
                    o = bank[H_BANKS[j % 4]][:, k * D:(k + 1) * D]
                    for h in range(H):
                        mm = nc.tensor.matmul(o, (xnT, zT)[l][:, h, (t + k) * P:(t + k + 1) * P], wc[:, l, 0, h, :], start=(h == 0), stop=(h == H - 1))
                mm.then_inc(pe_h, 1)

            def z_block(j, fo, b):
                for h in range(H):
                    mm = nc.tensor.matmul(bank[b][:, 0:WIDTH[j]], wc[:, l, 1, h, fo * P:(fo + 1) * P],
                                          aggT[:, h, 512 * j:512 * j + WIDTH[j]], start=(h == 0), stop=(h == H - 1))
                return mm

            def edges_to_partitions():
                pe.wait_ge(meta_rel, 1)
                for k in range(3):
                    for g in range(GROUPS):
                        a = relT[:, g, :] if k == 1 else metaF[:, k, g, :]
                        mm = nc.tensor.transpose(bank[k][:, g * P:(g + 1) * P], a, ident[:, :])
                mm.then_inc(p_ready, 1)
                for k in range(3):
                    for g in range(GROUPS):
                        a = farW[:, g, :] if k == 2 else metaF[:, k, g, :]
                        nc.tensor.matmul(bank[3][:, k * 32:k * 32 + CROSS], a, pick[:, g, :], start=(g == 0), stop=(g == GROUPS - 1))
                for g in range(GROUPS):
                    nc.tensor.matmul(bank[3][0:1, 24:25], nfar[:, g:g + 1], ones[:, 0:1], start=(g == 0), stop=(g == GROUPS - 1))
                for g in range(GROUPS):
                    mm = nc.tensor.matmul(bank[3][0:1, 96 + g * P:min(96 + (g + 1) * P, 512)], metaF[:, 1, g, 0:1],
                                          ident[:, 0:min(P, CHUNKS - g * P)], start=True, stop=True)
                mm.then_inc(pe_meta, 1)

            for j in range(NP + 2):
                if j == EDGES_AT:
                    edges_to_partitions()
                if j < NP:
                    rows_to_T(0, j)
                if j == 2:
                    pe.wait_ge(w1_in, 32)
                if j >= 2:
                    h_rows(0, j - 2)
            pe.wait_ge(tr_out, NP)
            pe.wait_ge(cols_in, 16 * 11)
            nc.tensor.transpose(bank[6][:, 0:P], colsrc, ident[:, :]).then_inc(pe_cols, 1)
            pe.wait_ge(small_in, 16 * 6)
            late = None
            for l in range(2):
                if l:
                    for j in range(NP):
                        h_rows(1, j)
                for n, (a, b) in enumerate(zip([0] + EARLY, EARLY + [ITER])):
                    with pe.Fori(a, b, 1) as i:
                        for q in range(4):
                            pe.wait_ge(s_ready, i * 4 + (l * (NGROUP + 1) + q + 1))
                            pe.wait_ge(acc_done, i * (4 * GROUP) + (l * ACC + (q + 1) * GROUP))
                            for k in range(GROUP):
                                j = q * GROUP + k
                                pe.wait_ge(got[j], i * 16 + 16 * (l * ITER + 1))
                                o = bank[2 * (q % 2) + k // 2]
                                for h in range(H):
                                    mm = nc.tensor.matmul(o[:, (k % 2) * 256 + h * P:(k % 2) * 256 + (h + 1) * P],
                                                          msgs[:, j, h * P:(h + 1) * P], S[:, (q % 2) * GROUP + k, :],
                                                          start=True, stop=True)
                            mm.then_inc(p_ready, 1)
                    if b < ITER:
                        pe.wait_ge(acc_done, l * ACC + ZEROED + b * BODY - GROUP)
                        for fo in range(H):
                            if n >= 2:
                                pe.wait_ge(z_out, l * NB * H + (n - 2) * H + fo + 1)
                            z_block(n, fo, 4 + (n * H + fo) % 4).then_inc(pe_z, 1)
                if late is None:
                    pe.wait_ge(late_ready, 1)
                    late = pe.value_load(late_i[0:1, 0:1], min_val=0, max_val=E + NB)
                pe.wait_ge(acc_done, (l + 1) * ACC)
                with pe.If(late > 0):
                    for g in range(XGROUP):
                        pe.wait_ge(x_s, l * XGROUP + g + 1)
                        pe.wait_ge(x_got, 16 * (l * CROSS + (g + 1) * GROUP))
                        if g:
                            pe.wait_ge(x_acc, l * CROSS + g * GROUP)
                        for k in range(GROUP):
                            u = g * GROUP + k
                            for h in range(H):
                                mm = nc.tensor.matmul(bank[k // 2][:, (k % 2) * 256 + h * P:(k % 2) * 256 + (h + 1) * P],
                                                      msgs[:, u % BODY, h * P:(h + 1) * P], S[:, k, :], start=True, stop=True)
                        mm.then_inc(x_p, 1)
                    pe.wait_ge(x_acc, (l + 1) * CROSS)
                    pe.wait_ge(z_out, l * NB * H + len(EARLY) * H)
                    for n in range(len(EARLY) * H):
                        if n:
                            pe.wait_ge(x_zout, l * len(EARLY) * H + n)
                        z_block(n // H, n % H, 4).then_inc(x_z, 1)
                    pe.wait_ge(x_zout, (l + 1) * len(EARLY) * H)
                for n in range(len(EARLY) * H, NB * H):
                    if n >= 4:
                        pe.wait_ge(z_out, l * NB * H + n - 3)
                    z_block(n // H, n % H, 4 + n % 4).then_inc(pe_z, 1)
                pe.wait_ge(z_out, (l + 1) * NB * H)
            for j, (t, w) in enumerate(PAIRS):
                need = min(NB, -(-(t + w) * P // 512))
                pe.wait_ge(act_in, (NB + need) * H)
                if j >= 4:
                    pe.wait_ge(x1_ready, j - 3)
                for k in range(w):
                    for h in range(H):
                        mm = nc.tensor.transpose(bank[BACK_BANKS[j % 4]][:, k * D + h * P:k * D + (h + 1) * P],
                                                 zT[:, h, (t + k) * P:(t + k + 1) * P], ident[:, :])
                mm.then_inc(pe_back, 1)
            for j in range(NP + 2):
                if j < NP:
                    rows_to_T(1, j)
                if j < 2:
                    continue
                j -= 2
                t, w = PAIRS[j]
                pe.wait_ge(tr_out, NP + j + 1)
                for k in range(w):
                    o = bank[2][:, (t + k) * NE:(t + k + 1) * NE]
                    for h in range(H):
                        mm = nc.tensor.matmul(o, aggT[:, h, (t + k) * P:(t + k + 1) * P], gw[:, h, :], start=(h == 0), stop=(h == H - 1))
            mm.then_inc(pe_gate, 1)
            pe.wait_ge(hot_ready, 1)
            hots = hot[:, :, :].rearrange("p t e -> p (t e)")
            nc.tensor.matmul(bank[3][:, 0:TILES * NE], upper[:, :], hots, start=True, stop=True)
            nc.tensor.matmul(bank[4][:, 0:TILES * NE], ones[:, :], hots, start=True, stop=True).then_inc(pe_rank, 1)

            def expert_in(e):
                pe.wait_ge(erow_in[e % 2], 16 * (e // 2 + 1))
                for h in range(H):
                    for s in range(ST):
                        mm = nc.tensor.transpose(bank[h][:, s * P:(s + 1) * P], erow[e % 2][:, s, h * P:(h + 1) * P], ident[:, :])
                mm.then_inc(pe_in, 1)

            expert_in(0)
            for e in range(NE):
                pe.wait_ge(in_out, e + 1)
                pe.wait_ge(w_in[e % 2], 48 * (e // 2 + 1))
                for f in range(FT):
                    n = e * FT + f
                    if n >= 3:
                        pe.wait_ge(hid_out, n - 2)
                    for h in range(H):
                        mm = nc.tensor.matmul(bank[2 + n % 3][:, 0:CAP], we1[:, e % 2, h, f * P:(f + 1) * P], inT[e % 2][:, h, 0:CAP],
                                              start=(h == 0), stop=(h == H - 1))
                    mm.then_inc(pe_hid, 1)
                if e + 1 < NE:
                    expert_in(e + 1)
                pe.wait_ge(hid_out, (e + 1) * FT)
                for s in range(ST):
                    n = e * ST + s
                    if n >= 3:
                        pe.wait_ge(y_read, n - 2)
                    o = bank[5 + n % 3][:, 0:D]
                    for f in range(FT):
                        mm = nc.tensor.matmul(o, hid[e % 2][:, f, s * P:(s + 1) * P], we2[:, e % 2, f, :], start=(f == 0), stop=(f == FT - 1))
                    mm.then_inc(pe_y, 1)

        @block.scalar
        def _(act):
            def layernorm_sqrt(n, g):
                a, b = XG[g]
                act.wait_ge(var_ready, n * len(XG) + g + 1)
                nc.scalar.activation(sq[:, a:b], sd[:, a:b], ACT.Sqrt).then_inc(sqrt_done, 1)

            def T_out(n, to, j):
                t, w = PAIRS[j]
                act.wait_ge(pe_tr, n * NP + j + 1)
                nc.scalar.copy(to[:, :, t * P:(t + w) * P],
                               bank[T_BANKS[n][j % len(T_BANKS[n])]][:, :].rearrange("p (h n) -> p h n", h=H)[:, :, 0:w * P]).then_inc(tr_out, 1)

            def h_rows_out(l, j):
                t, w = PAIRS[j]
                act.wait_ge(h_sum, l * NP + j + 1)
                nc.scalar.activation(rows[:, t:t + w, 0:D], rows[:, t:t + w, 0:D], ACT.Relu).then_inc(h_out, 1)

            def z_out_block(j, fo, b):
                return nc.scalar.activation(zT[:, fo, 512 * j:512 * j + WIDTH[j]], bank[b][:, 0:WIDTH[j]], ACT.Identity,
                                            bias=vec(l, B2, fo))

            def norm_pairs(n, each):
                layernorm_sqrt(n, 0)
                for g, (a, b) in enumerate(XG):
                    act.wait_ge(norm_coef, n * len(XG) + g + 1)
                    for j in range(a // 2, -(-b // 2)):
                        if j == -(-b // 2) - 1:
                            if g + 1 < len(XG):
                                layernorm_sqrt(n, g + 1)
                            elif n:
                                nc.scalar.activation(warm[:, :], sq[:, 0:1], ACT.Exp)
                        for t in range(2 * j, min(2 * j + 2, b)):
                            nc.scalar.activation(rows[:, t, 0:D], rows[:, t, D:2 * D], ACT.Identity, bias=nmr[:, t:t + 1],
                                                 scale=rs[:, t:t + 1]).then_inc(rows_norm, 1)
                        each(j)

            def stage(b, c0):
                nc.scalar.copy(idx_now[:, b, :], metaE[:, 0, bass.ds(c0, BLOCK)])
                nc.scalar.copy(relw_now[:, b, :, :], metaE[:, 1:3, bass.ds(c0, BLOCK)]).then_inc(staged, 1)

            act.dma_start(rows[:, 0:XG[0][1], D:2 * D], xt[:, 0:XG[0][1], :]).then_inc(x_in[0], 16)
            act.dma_start(wc[:, 0, 0], conv[0]["w1"].rearrange("(h p) n -> p h n", p=P)).then_inc(w1_in, 16)
            act.dma_start(b1row[:, 0, :], conv[0]["b1"].rearrange("(a n) -> a n", a=1).partition_broadcast(P)).then_inc(w1_in, 16)

            def first_pair(j):
                if j == 0:
                    act.wait_ge(meta_in, 16 * 9)
                    nc.scalar.copy(metaF[:, 0:2], metaI[:, :]).then_inc(meta_f, 1)
                if j == EDGES_AT + 1:
                    act.wait_ge(pe_meta, 1)
                    act.wait_ge(pads, 2)
                    for k in range(3):
                        nc.scalar.copy(metaE[:, k, 0:CHUNKS], bank[k][:, 0:CHUNKS]).then_inc(metaE_done, 1)
                if j >= 2:
                    T_out(0, xnT, j - 2)
                if j >= 4:
                    h_rows_out(0, j - 4)

            norm_pairs(0, first_pair)
            for j in range(NP, NP + 4):
                if j < NP + 2:
                    T_out(0, xnT, j - 2)
                h_rows_out(0, j - 4)
            act.wait_ge(pe_cols, 1)
            nc.scalar.copy(cols[:, :], bank[6][:, 0:P]).then_inc(cols_done, 1)
            late = None
            for l in range(2):
                if l:
                    for j in range(NP):
                        h_rows_out(1, j)
                act.wait_ge(metaE_done, 4)
                stage(0, 0)
                stage(1, BLOCK)
                ends = [e + 1 for e in EARLY]
                for n, (a, b) in enumerate(zip([0] + ends, ends + [ITER - 1])):
                    with act.Fori(a, b, 1) as i:
                        for k in range(2):
                            act.wait_ge(acc_done, i * BODY + (l * ACC + ZEROED + (k + 1) * BLOCK))
                            stage(k, i * BODY + (k + 2) * BLOCK)
                    if n < len(EARLY):
                        for fo in range(H):
                            act.wait_ge(pe_z, l * NB * H + n * H + fo + 1)
                            z_out_block(n, fo, 4 + (n * H + fo) % 4).then_inc(z_out, 1)
                act.wait_ge(acc_done, l * ACC + ZEROED + (BLOCKS - 1) * BLOCK)
                stage(0, CHUNKS)
                if late is None:
                    act.wait_ge(late_ready, 1)
                    late = act.value_load(late_i[0:1, 0:1], min_val=0, max_val=E + NB)
                with act.If(late > 0):
                    for n in range(len(EARLY) * H):
                        act.wait_ge(x_z, l * len(EARLY) * H + n + 1)
                        z_out_block(n // H, n % H, 4).then_inc(x_zout, 1)
                for n in range(len(EARLY) * H, NB * H):
                    act.wait_ge(pe_z, l * NB * H + n + 1)
                    z_out_block(n // H, n % H, 4 + n % 4).then_inc(z_out, 1)
                for k in range(2):
                    act.wait_ge(bvar_ready, 2 * l + k + 1)
                    nc.scalar.activation(bsq[:, :], bsd[:, :], ACT.Sqrt).then_inc(bsqrt_done, 1)
                    act.wait_ge(coef_ready, 2 * l + k + 1)
                    for n in range(NB * H):
                        j, fo = divmod(n, H)
                        a = zT[:, fo, 512 * j:512 * j + WIDTH[j]]
                        if k == 0:
                            nc.scalar.activation(a, a, ACT.Relu, bias=bof[:, fo:fo + 1], scale=bsc[:, fo:fo + 1]).then_inc(y_out, 1)
                        elif l == 0:
                            nc.scalar.activation(a, a, ACT.Relu, bias=bof[:, fo:fo + 1], scale=bsc[:, fo:fo + 1]).then_inc(act_in, 1)
                        else:
                            act.wait_ge(res_mul, n + 1)
                            nc.scalar.activation(a, a, ACT.Relu, bias=bof[:, fo:fo + 1]).then_inc(act_in, 1)
            act.wait_ge(h_stored, 16 * STORES * 2)
            norm_pairs(1, lambda j: T_out(1, aggT, j - 2) if j >= 2 else None)
            for j in range(NP - 2, NP):
                T_out(1, aggT, j)
            act.wait_ge(lg_ready, 1)
            nc.scalar.activation(ex[:, :, :], lg[:, :, :], ACT.Exp).then_inc(exp_done, 1)
            for e in range(NE):
                act.wait_ge(pe_in, e + 1)
                if e >= 2:
                    act.wait_ge(pe_y, ST * (e - 1))
                for h in range(H):
                    c = nc.scalar.copy(inT[e % 2][:, h, :], bank[h][:, :])
                c.then_inc(in_out, 1)
                for f in range(FT):
                    n = e * FT + f
                    act.wait_ge(pe_hid, n + 1)
                    nc.scalar.activation(hid[e % 2][:, f, 0:CAP], bank[2 + n % 3][:, 0:CAP], ACT.Relu,
                                         bias=expert_bias(e, f)).then_inc(hid_out, 1)

        @block.vector
        def _(dve):
            chain = [0]

            def then(ins):
                chain[0] += 1
                ins.then_inc(dve_chain, 1)
                dve.wait_ge(dve_chain, chain[0])

            def layernorm(n, g, arrived):
                a, b = XG[g]
                for t in range(a, b):
                    arrived(t)
                    c = nc.vector.bn_stats(st[:, t, :], rows[:, t, D:2 * D])
                then(c)
                for t in range(a, b):
                    c = nc.vector.bn_aggr(mv[:, t, :], st[:, t, :])
                then(c)
                nc.vector.tensor_scalar(sd[:, a:b], mv[:, a:b, 1], EPS, None, ALU.add).then_inc(var_ready, 1)

            def layernorm_coef(n, g):
                a, b = XG[g]
                dve.wait_ge(sqrt_done, n * len(XG) + g + 1)
                then(nc.vector.reciprocal(rs[:, a:b], sq[:, a:b]))
                nc.vector.scalar_tensor_tensor(out=nmr[:, a:b], in0=mv[:, a:b, 0], scalar=-1.0, in1=rs[:, a:b],
                                               op0=ALU.mult, op1=ALU.mult).then_inc(norm_coef, 1)

            def h_plus_bias(l, j):
                t, w = PAIRS[j]
                dve.wait_ge(pe_h, l * NP + j + 1)
                nc.vector.tensor_tensor(rows[:, t:t + w, 0:D], bank[H_BANKS[j % 4]][:, 0:w * D].rearrange("p (t d) -> p t d", t=w),
                                        b1row[:, l:l + 1, :].broadcast_to([P, w, D]), ALU.add).then_inc(h_sum, 1)

            nc.vector.memset(rows[:, TILES - 1, D:2 * D], 0.0).then_inc(tail_zero, 1)

            def edges_prepared():
                dve.wait_ge(consts, 10)
                nc.vector.tensor_copy(iota_f[:, :], iota_i[:, :])
                nc.vector.tensor_copy(rank[:, :], rank_i[:, :])
                nc.vector.tensor_copy(base[:, :], base_i[:, :])
                nc.vector.tensor_copy(tok_f[:, :], tok_i[:, :])
                nc.vector.tensor_copy(rows[:, :, 2 * D].bitcast(I32), tok_i[:, :])
                then(nc.vector.tensor_copy(bound[:, :], bound_i[:, :]))
                dve.wait_ge(meta_f, 1)
                for g in range(GROUPS):
                    nc.vector.tensor_scalar(gt_first[:, g, :], bound[:, :], metaF[:, 1, g, 0:1], None, ALU.is_gt)
                    c = nc.vector.tensor_scalar(relT[:, g, :], metaF[:, 1, g, :], metaF[:, 1, g, 0:1], None, ALU.subtract)
                then(c)
                for g in range(GROUPS):
                    nc.vector.scalar_tensor_tensor(out=pick[:, g, :], in0=bound[:, :], scalar=metaF[:, 1, g, P - 1:P],
                                                   in1=gt_first[:, g, :], op0=ALU.is_le, op1=ALU.mult)
                nc.vector.tensor_scalar(farW, metaF[:, 2], 0.0, None, ALU.not_equal)
                then(nc.vector.tensor_scalar(far, relT, float(P), None, ALU.is_ge))
                then(nc.vector.tensor_tensor(farW, farW, far, ALU.mult))
                then(nc.vector.tensor_reduce(nfar[:, :], farW, AX_X, ALU.add))
                nc.vector.tensor_tensor(farW, metaF[:, 2], far, ALU.mult).then_inc(meta_rel, 1)

            def edges_placed():
                dve.wait_ge(pe_meta, 1)
                nc.vector.tensor_copy(idx_x[:, :], bank[3][:, 0:CROSS])
                nc.vector.tensor_tensor(metaX[:, 1, :], bank[3][:, 32:32 + CROSS], bound[:, :], ALU.subtract)
                nc.vector.tensor_copy(metaX[:, 2, :], bank[3][:, 64:64 + CROSS])
                nc.vector.tensor_copy(late_f[:, NB:], bank[3][0:1, 24:25])
                nc.vector.tensor_copy(offs[:, :], bank[3][0:1, 96:96 + CHUNKS])
                nc.vector.tensor_copy(offs_f[:, :], bank[3][0:1, 96:96 + CHUNKS]).then_inc(metaE_done, 1)

            def x_arrived(t):
                g = next(g for g, (a, b) in enumerate(XG) if a <= t < b)
                if XG[g][0] == t:
                    dve.wait_ge(x_in[g], 32 if XG[g][1] == TILES else 16)

            dve.wait_ge(consts, 10)
            adds = {3: range(1, 3), 4: range(3, 6)}
            for g in range(len(XG)):
                layernorm(0, g, x_arrived)
                for j in adds.get(g, ()):
                    h_plus_bias(0, j)
                layernorm_coef(0, g)
                if g == 1:
                    edges_prepared()
                elif g == 2:
                    h_plus_bias(0, 0)
            for j in range(6, NP):
                h_plus_bias(0, j)
                if j == 6:
                    edges_placed()
            dve.wait_ge(metaE_done, 4)
            nc.vector.memset(late_f[:, len(EARLY):NB], 0.0)
            for j, i in enumerate(EARLY):
                c = nc.vector.tensor_scalar(late_f[:, j:j + 1], offs_f[:, i * BODY - GROUP:i * BODY - GROUP + 1], 512.0 * (j + 1), None, ALU.is_lt)
            then(c)
            then(nc.vector.tensor_reduce(late_f[:, 0:1], late_f[:, :], AX_X, ALU.add))
            nc.vector.tensor_copy(late_i[:, :], late_f[:, 0:1]).then_inc(late_ready, 1)
            dve.wait_ge(late_ready, 1)
            late = dve.value_load(late_i[0:1, 0:1], min_val=0, max_val=E + NB)

            def build_S(half, q):
                b, c0 = (q // 2) % 2, (q % 2) * GROUP
                for k in range(GROUP):
                    c = nc.vector.tensor_scalar(S[:, half * GROUP + k, :], iota_f[:, :], relw_now[:, b, 0, c0 + k:c0 + k + 1],
                                                relw_now[:, b, 1, c0 + k:c0 + k + 1], ALU.is_equal, ALU.mult)
                c.then_inc(s_ready, 1)

            def stats(j, fo):
                return nc.vector.bn_stats(bst[:, fo, j, :], zT[:, fo, 512 * j:512 * j + WIDTH[j]])

            for l in range(2):
                if l:
                    for j in range(NP):
                        h_plus_bias(1, j)
                else:
                    dve.wait_ge(cols_done, 1)
                dve.wait_ge(staged, l * (BLOCKS + 1) + 1)
                build_S(0, 0)
                ends = [e + 2 for e in EARLY]
                for n, (a, b) in enumerate(zip([0] + ends, ends + [ITER])):
                    with dve.Fori(a, b, 1) as i:
                        for q in range(4):
                            dve.wait_ge(p_ready, i * 4 + (l * NGROUP + q + 1))
                            if q % 2:
                                dve.wait_ge(staged, i * 2 + (l * (BLOCKS + 1) + (q + 1) // 2 + 1))
                            build_S((q + 1) % 2, q + 1)
                            _, at = nc.values_load_multi_w_load_instructions(
                                offs[0:1, bass.ds(i * BODY + q * GROUP, GROUP)], engines=[mybir.EngineType.DVE],
                                min_val=0, max_val=N - 1, skip_runtime_bounds_check_because="dst lies in [0, N)")
                            dve.wait_ge(p_ready, i * 4 + (l * NGROUP + q + 2))
                            for k in range(GROUP):
                                dve.wait_ge(acc_done, i * BODY + (l * ACC + ZEROED + q * GROUP + k))
                                a = aggT[:, :, bass.ds(at[k], P)]
                                o = bank[2 * (q % 2) + k // 2][:, (k % 2) * 256:(k % 2 + 1) * 256].rearrange("p (h n) -> p h n", h=H)
                                nc.vector.tensor_tensor(a, a, o, ALU.add).then_inc(acc_done, 1)
                    if n < len(EARLY):
                        for fo in range(H):
                            dve.wait_ge(z_out, l * NB * H + n * H + fo + 1)
                            stats(n, fo)
                with dve.If(late > 0):
                    dve.wait_ge(acc_done, (l + 1) * ACC)
                    for g in range(XGROUP):
                        if g:
                            dve.wait_ge(x_p, l * XGROUP + g)
                        for k in range(GROUP):
                            u = g * GROUP + k
                            c = nc.vector.tensor_scalar(S[:, k, :], iota_f[:, :], metaX[:, 1, u:u + 1], metaX[:, 2, u:u + 1],
                                                        ALU.is_equal, ALU.mult)
                        c.then_inc(x_s, 1)
                        dve.wait_ge(x_p, l * XGROUP + g + 1)
                        for k in range(GROUP):
                            u = g * GROUP + k
                            a = aggT[:, :, (u + 1) * P:(u + 2) * P]
                            o = bank[k // 2][:, (k % 2) * 256:(k % 2 + 1) * 256].rearrange("p (h n) -> p h n", h=H)
                            nc.vector.tensor_tensor(a, a, o, ALU.add).then_inc(x_acc, 1)
                    for n in range(len(EARLY) * H):
                        dve.wait_ge(x_zout, l * len(EARLY) * H + n + 1)
                        stats(n // H, n % H)

                for k in range(2):
                    for n in range(0 if k else len(EARLY) * H, NB * H):
                        dve.wait_ge(y_out if k else z_out, l * NB * H + n + 1)
                        c = stats(n // H, n % H)
                    then(c)
                    for fo in range(H):
                        c = nc.vector.bn_aggr(bmv[:, fo, :], bst[:, fo, :, :].rearrange("p j s -> p (j s)"))
                    then(c)
                    nc.vector.tensor_scalar(bsd[:, :], bmv[:, :, 1], EPS, None, ALU.add).then_inc(bvar_ready, 1)
                    dve.wait_ge(bsqrt_done, 2 * l + k + 1)
                    then(nc.vector.reciprocal(brs[:, :], bsq[:, :]))
                    then(nc.vector.tensor_tensor(bsc[:, :], brs[:, :], vec(l, (G, BNG)[k]), ALU.mult))
                    then(nc.vector.tensor_tensor(bms[:, :], bmv[:, :, 0], bsc[:, :], ALU.mult))
                    nc.vector.tensor_tensor(bof[:, :], vec(l, (B, BNB)[k]), bms[:, :], ALU.subtract).then_inc(coef_ready, 1)
            dve.wait_ge(coef_ready, 4)
            for n in range(NB * H):
                j, fo = divmod(n, H)
                a = zT[:, fo, 512 * j:512 * j + WIDTH[j]]
                nc.vector.scalar_tensor_tensor(out=a, in0=a, scalar=bsc[:, fo:fo + 1], in1=xnT[:, fo, 512 * j:512 * j + WIDTH[j]],
                                               op0=ALU.mult, op1=ALU.add).then_inc(res_mul, 1)
            done = 0
            for g, (a, b) in enumerate(XG):
                for j in range(done, -(-b // 2)):
                    t, w = PAIRS[j]
                    dve.wait_ge(pe_back, j + 1)
                    nc.vector.tensor_tensor(rows[:, t:t + w, D:2 * D], rows[:, t:t + w, D:2 * D],
                                            bank[BACK_BANKS[j % 4]][:, 0:w * D].rearrange("p (t d) -> p t d", t=w), ALU.add).then_inc(x1_ready, 1)
                done = -(-b // 2)
                layernorm(1, g, lambda t: dve.wait_ge(x1_ready, t // 2 + 1))
                if g:
                    layernorm_coef(1, g - 1)
            layernorm_coef(1, len(XG) - 1)
            dve.wait_ge(pe_gate, 1)
            L = bank[2][:, 0:TILES * NE].rearrange("p (t e) -> p t e", e=NE)

            def wide(a):
                return a[:, :].rearrange("p (t o) -> p t o", o=1).broadcast_to([P, TILES, NE])

            def each(a):
                return a[:, :].rearrange("p (o e) -> p o e", o=1).broadcast_to([P, TILES, NE])

            then(nc.vector.tensor_tensor(lg[:, :, :], L, each(gb), ALU.add))
            then(nc.vector.tensor_reduce(r1[:, :], lg[:, :, :], AX_X, ALU.max))
            nc.vector.tensor_tensor(lg[:, :, :], lg[:, :, :], wide(r1), ALU.subtract).then_inc(lg_ready, 1)
            dve.wait_ge(exp_done, 1)
            nc.vector.tensor_reduce(r1[:, :], ex[:, :, :], AX_X, ALU.max)
            then(nc.vector.tensor_reduce(r2[:, :], ex[:, :, :], AX_X, ALU.add))
            then(nc.vector.reciprocal(r3[:, :], r2[:, :]))
            nc.vector.tensor_tensor(rows[:, :, 2 * D + 1], r1[:, :], r3[:, :], ALU.mult)
            then(nc.vector.tensor_tensor(hot[:, :, :], ex[:, :, :], wide(r1), ALU.is_equal))
            then(nc.vector.tensor_tensor(hot[:, :, :], hot[:, :, :], each(rank), ALU.mult))
            then(nc.vector.tensor_reduce(r2[:, :], hot[:, :, :], AX_X, ALU.max))
            then(nc.vector.tensor_tensor(hot[:, :, :], hot[:, :, :], wide(r2), ALU.is_equal))
            then(nc.vector.tensor_scalar(r3[:, :], tok_f[:, :], float(N), None, ALU.is_lt))
            nc.vector.tensor_tensor(hot[:, :, :], hot[:, :, :], wide(r3), ALU.mult).then_inc(hot_ready, 1)
            dve.wait_ge(pe_rank, 1)
            then(nc.vector.tensor_copy(tot[:, :, :].rearrange("p t e -> p (t e)"), bank[4][:, 0:TILES * NE]))
            nc.vector.memset(cum[:, 0, :], 0.0)
            then(nc.vector.tensor_copy(cum[:, 1:, :], tot[:, :TILES - 1, :]))
            a, b, step = cum, tot, 1
            while step < TILES:
                nc.vector.tensor_copy(b[:, 0:step, :], a[:, 0:step, :])
                then(nc.vector.tensor_tensor(b[:, step:, :], a[:, step:, :], a[:, :TILES - step, :], ALU.add))
                a, b, step = b, a, 2 * step
            before = a
            then(nc.vector.tensor_tensor(cum[:, :, :], before[:, :, :], bank[3][:, 0:TILES * NE].rearrange("p (t e) -> p t e", e=NE), ALU.add))
            nc.vector.tensor_tensor(tot[:, :, :], hot[:, :, :], each(base), ALU.mult)
            then(nc.vector.tensor_tensor(cum[:, :, :], cum[:, :, :], hot[:, :, :], ALU.mult))
            nc.vector.tensor_reduce(r1[:, :], cum[:, :, :], AX_X, ALU.add)
            then(nc.vector.tensor_reduce(r2[:, :], tot[:, :, :], AX_X, ALU.add))
            nc.vector.tensor_scalar(r4[:, :], r1[:, :], float(CAP), float(FAR), ALU.is_gt, ALU.mult)
            then(nc.vector.scalar_tensor_tensor(out=r2[:, :], in0=r1[:, :], scalar=-1.0, in1=r2[:, :], op0=ALU.add, op1=ALU.add))
            nc.vector.tensor_scalar(r3[:, :], r3[:, :], -float(FAR), float(FAR), ALU.mult, ALU.add)
            then(nc.vector.tensor_tensor(r2[:, :], r2[:, :], r4[:, :], ALU.add))
            nc.vector.tensor_tensor(slot_i[:, :], r2[:, :], r3[:, :], ALU.add).then_inc(slots_ready, 1)

            for i in range(NE * ST):
                e, s = divmod(i, ST)
                er = erow[e % 2]
                dve.wait_ge(pe_y, i + 1)
                nc.vector.tensor_tensor(yv, bank[5 + i % 3][:, 0:D], be2[:, e % 2, :], ALU.add).then_inc(y_read, 1)
                dve.wait_ge(y_read, i + 1)
                then(nc.vector.tensor_scalar(yv, yv, er[:, s, 2 * D + 1:2 * D + 2], None, ALU.mult))
                nc.vector.tensor_tensor(ymask, yv, yv, ALU.subtract)
                nc.vector.tensor_scalar(ya, yv, FLT_MAX, NAN_TO_NUM_INF, ALU.is_gt, ALU.mult)
                if i >= 4:
                    dve.wait_ge(y_sent[i % 4], 16 * (i // 4))
                then(nc.vector.tensor_scalar(yo[:, i % 4, :], yv, -FLT_MAX, -NAN_TO_NUM_INF, ALU.is_lt, ALU.mult))
                then(nc.vector.tensor_tensor(ya, ya, yo[:, i % 4, :], ALU.add))
                then(nc.vector.copy_predicated(yv, ymask.bitcast(U32), ya))
                nc.vector.tensor_tensor(yo[:, i % 4, :], yv, er[:, s, D:2 * D], ALU.add).then_inc(y_ready, 1)
                dve.wait_ge(y_ready, i + 1)


_INS = ["x", "src", "dst", "edge_weight"] + [f"L0_gnn_{k}" for k in (
    "c1_w1", "c1_b1", "c1_w2", "c1_b2", "c1_g", "c1_b", "bn1_g", "bn1_b",
    "c2_w1", "c2_b1", "c2_w2", "c2_b2", "c2_g", "c2_b", "bn2_g", "bn2_b")] + [
    f"L0_ffn_{k}" for k in ("gate_w", "gate_b", "w1", "b1", "w2", "b2")]


def build(nc, ap, out):
    conv = []
    for l in (1, 2):
        c = {k: ap[f"L0_gnn_c{l}_{k}"] for k in ("w1", "b1", "w2", "b2", "g", "b")}
        c["bng"], c["bnb"] = ap[f"L0_gnn_bn{l}_g"], ap[f"L0_gnn_bn{l}_b"]
        conv.append(c)
    f = {k: ap[f"L0_ffn_{k}"] for k in ("gate_w", "gate_b", "w1", "b1", "w2", "b2")}
    gnn_moe_program(nc, ap["x"], ap["src"], ap["dst"], ap["edge_weight"], conv, f["gate_w"], f["gate_b"],
                    f["w1"], f["b1"], f["w2"], f["b2"], out)


def kernel(**inputs):
    import numpy as _np
    import concourse.bacc as _bacc
    from concourse.bass_utils import run_bass_kernel_spmd as _run

    nc = _bacc.Bacc("TRN2", target_bir_lowering=False, num_devices=1)
    arrays, aps = {}, {}
    for name in _INS:
        a = _np.ascontiguousarray(inputs[name])
        arrays[f"in_{name}"] = a
        aps[name] = nc.dram_tensor(f"in_{name}", a.shape, mybir.dt.from_np(a.dtype), kind="ExternalInput").ap()
    out = nc.dram_tensor("out_x", arrays["in_x"].shape, F32, kind="ExternalOutput").ap()
    build(nc, aps, out)
    r = _run(nc, [arrays], core_ids=[0])
    return r.results[0]["out_x"]
```

```python
from contextlib import ExitStack

import numpy as np

import concourse.bass as bass
from concourse import mybir

F32 = mybir.dt.float32
F32R = mybir.dt.float32r
I32 = mybir.dt.int32
U32 = mybir.dt.uint32
ALU = mybir.AluOpType
ACT = mybir.ActivationFunctionType
AX_X = mybir.AxisListType.X

P = 128
EPS = 1e-5
FLT_MAX = float(np.finfo(np.float32).max)
NAN_TO_NUM_INF = 1e4


def gnn_moe_program(nc, x, src, dst, ew, conv, gate_w, gate_b, w1, b1, w2, b2, out):
    N, D = x.shape
    (E,) = src.shape
    NE, _, F = w1.shape
    H = D // P
    TILES = -(-N // P)
    TAIL = N - (TILES - 1) * P
    NPAD = TILES * P
    CHUNKS = -(-E // P)
    GROUPS = -(-CHUNKS // P)
    CROSS = TILES - 1
    BLOCK = 8
    GROUP = 4
    BODY = 2 * BLOCK
    ITER = CHUNKS // BODY
    BLOCKS = CHUNKS // BLOCK
    NGROUP = CHUNKS // GROUP
    XGROUP = CROSS // GROUP
    assert CROSS <= 24 and 96 + CHUNKS <= 512
    assert CHUNKS % BODY == 0 and CROSS % GROUP == 0 and H == 2
    def chunks_by(node):
        return -(-CHUNKS * node // N) + 8 + GROUP

    START, EARLY = [0], []
    while chunks_by(START[-1] + 512) <= (ITER - 2) * BODY:
        START.append(START[-1] + 512)
        EARLY.append(-(-chunks_by(START[-1]) // BODY))
    more = ((ITER - 2) * BODY - 8 - GROUP - 1) * N // CHUNKS
    if more > START[-1]:
        START.append(more)
        EARLY.append(ITER - 2)
    START += list(range(START[-1] + 512, N, 512)) + [N]
    NB = len(START) - 1
    FT = F // P
    CAP = max(1, -(-5 * N // (4 * NE)))
    USED = CAP + CAP % 2
    ESLOT = 512
    ST = ESLOT // P
    ROW = 2 * D + 2
    FAR = 1 << 20
    assert CAP <= ESLOT and ST == 4 and NE % 2 == 0 and NE >= 6
    SPLIT = 12
    XG = [(0, 4), (4, 10), (10, 16), (16, 22), (22, TILES)]
    assert SPLIT % 4 == 0 and XG[3][0] % 4 == 0 and SPLIT <= XG[3][0] < TILES

    h_dram = [nc.dram_tensor(f"h{l}", (N, D), F32, kind="Internal").ap() for l in range(2)]
    ebuf = nc.dram_tensor("expert_rows", (NE * ESLOT, ROW), F32, kind="Internal").ap()

    with ExitStack() as ctx:
        def sb(name, shape, dt=F32):
            return ctx.enter_context(nc.sbuf_tensor(name, shape, dt))

        def sem(name):
            return ctx.enter_context(nc.semaphore(name))

        rows = sb("rows", [P, TILES, ROW])
        msgs = sb("msgs", [P, BODY, D])
        S = sb("S", [P, 2 * GROUP, P])
        metaE = sb("metaE", [P, 3, CHUNKS + BLOCK])
        metaX = sb("metaX", [P, 3, CROSS])
        idx_x = sb("idx_x", [P, CROSS], I32)
        idx_now = sb("idx_now", [P, 2, BLOCK], I32)
        relw_now = sb("relw_now", [P, 2, 2, BLOCK])
        offs_f = sb("offs_f", [1, CHUNKS])
        offs = sb("offs", [1, CHUNKS], I32)
        late_f = sb("late_f", [1, NB + 1])
        late_i = sb("late_i", [1, 1], I32)
        iota_i = sb("iota_i", [P, P], I32)
        iota_f = sb("iota_f", [P, P])
        bound_i = sb("bound_i", [P, CROSS], I32)
        bound = sb("bound", [P, CROSS])
        nfar = sb("nfar", [P, GROUPS])
        ident = sb("ident", [P, P])
        upper = sb("upper", [P, P])
        ones = sb("ones", [P, P])
        wc = sb("wc", [P, 2, 2, H, D])
        b1row = sb("b1row", [P, 2, D])
        colsrc = S[:, 2 * GROUP - 1, :]
        cols = sb("cols", [P, P])
        gw = sb("gw", [P, H, NE])
        gb = sb("gb", [NE, 1])
        lgT = sb("lgT", [NE, NPAD])
        we1 = sb("we1", [P, H, F])
        we2 = sb("we2", [P, FT, D])
        be2 = sb("be2", [P, 2, D])
        st = sb("st", [P, TILES, 6])
        mv = sb("mv", [P, TILES, 2])
        sd = sb("sd", [P, TILES])
        sq = sb("sq", [P, TILES])
        rs = sb("rs", [P, TILES])
        nmr = sb("nmr", [P, TILES])
        bst = sb("bst", [P, H, NB, 6])
        bmv = sb("bmv", [P, H, 2])
        bsd = sb("bsd", [P, H])
        bsq = sb("bsq", [P, H])
        brs = sb("brs", [P, H])
        bsc = sb("bsc", [P, H])
        bms = sb("bms", [P, H])
        bof = sb("bof", [P, H])
        rank_i = sb("rank_i", [P, NE], I32)
        rank = sb("rank", [P, NE])
        base_i = sb("base_i", [P, NE], I32)
        base = sb("base", [P, NE])
        keep = sb("keep", [P, NE, SPLIT])
        invalid = sb("invalid", [P, TILES])
        valid = sb("valid", [P, 1])
        keep1 = sb("keep1", [P, NE, TILES - SPLIT])
        carry = sb("carry", [P, NE])
        r1 = sb("r1", [P, TILES])
        r2 = sb("r2", [P, TILES])
        r3 = sb("r3", [P, TILES])
        r4 = sb("r4", [P, TILES])
        tok_i = sb("tok_i", [P, TILES], I32)
        tok_f = sb("tok_f", [P, TILES])
        slot_i = sb("slot_i", [P, TILES], I32)

        with ExitStack() as gnn:
            xnT = gnn.enter_context(nc.sbuf_tensor("xnT", [P, H, NPAD], F32))
            aggT = gnn.enter_context(nc.sbuf_tensor("aggT", [P, H, NPAD + P], F32))
            zT = gnn.enter_context(nc.sbuf_tensor("zT", [P, H, NPAD], F32))
        w1h, w1l = (sb(name, [P, H, F], F32R) for name in ("w1h", "w1l"))
        w2h, w2l = (sb(name, [P, FT, D], F32R) for name in ("w2h", "w2l"))
        hidh, hidl = (sb(name, [P, FT, ESLOT], F32R) for name in ("hidh", "hidl"))
        inh, inl = (sb(name, [P, H, USED], F32R) for name in ("inh", "inl"))
        edges = aggT[:, :, :].rearrange("p h n -> p (h n)")
        GE = GROUPS * P
        metaI = edges[:, 0:2 * GE].bitcast(I32).rearrange("p (k g e) -> p k g e", k=2, e=P)
        metaF = edges[:, 2 * GE:5 * GE].rearrange("p (k g e) -> p k g e", k=3, e=P)
        relT = edges[:, 5 * GE:6 * GE].rearrange("p (g e) -> p g e", e=P)
        gt_first, pick = (
            edges[:, 6 * GE + P + k * GROUPS * CROSS:6 * GE + P + (k + 1) * GROUPS * CROSS].rearrange("p (g u) -> p g u", g=GROUPS)
            for k in range(2))
        farW = edges[:, 7 * GE:8 * GE].rearrange("p (g e) -> p g e", e=P)
        far = edges[:, 8 * GE:9 * GE].rearrange("p (g e) -> p g e", e=P)
        PARTS = [(0, SPLIT), (SPLIT, TILES)]
        at = [0]

        def tables(a, b):
            t = []
            for _ in range(6):
                at[0] += NE * (b - a)
                t.append(xnT[:, 1, NPAD - at[0]:NPAD - at[0] + NE * (b - a)].rearrange("p (e t) -> p e t", e=NE))
            return t

        gate_tables = [tables(a, b) for a, b in PARTS]
        flat = rows[:, :, :].rearrange("p t r -> p (t r)")
        REST = ROW - D
        erow, erest = ([flat[:, a + i * ST * w:a + (i + 1) * ST * w].rearrange("p (s r) -> p s r", s=ST) for i in range(2)]
                       for a, w in ((0, D), (2 * ST * D, REST)))
        yv, ymask, ya = (flat[:, 2 * ST * ROW + i * 2 * D:2 * ST * ROW + (i + 1) * 2 * D].rearrange("p (s d) -> p s d", s=2)
                         for i in range(3))
        yo = msgs[:, 0:ST, :]
        hidf = msgs[:, ST:, :].rearrange("p j d -> p (j d)")[:, 0:4 * USED].rearrange("p (i s) -> p i s", i=4)
        fill = we1[:, 0, 0:ROW]

        keeps = [k[:, :, :].rearrange("p e t -> p (e t)") for k in (keep, keep1)]

        bank = [ctx.enter_context(nc.psum_tensor(f"bank{i}", [P, 512], F32)) for i in range(8)]

        x_in = [sem(f"x_in{g}") for g in range(len(XG))]
        meta_zero = sem("meta_zero")
        meta_in = sem("meta_in")
        w1_in = sem("w1_in")
        small_in = sem("small_in")
        consts = sem("consts")
        pads = sem("pads")
        tail_zero = sem("tail_zero")
        fill_ready = sem("fill_ready")
        filled = sem("filled")
        dve_chain = sem("dve_chain")
        meta_f = sem("meta_f")
        meta_rel = sem("meta_rel")
        pe_meta = sem("pe_meta")
        metaE_done = sem("metaE_done")
        cols_in = sem("cols_in")
        pe_cols = sem("pe_cols")
        cols_done = sem("cols_done")
        norm_coef = sem("norm_coef")
        h_sum = sem("h_sum")
        var_ready = sem("var_ready")
        sqrt_done = sem("sqrt_done")
        rows_norm = sem("rows_norm")
        rows_norm_v = sem("rows_norm_v")
        pe_tr = sem("pe_tr")
        tr_out = sem("tr_out")
        pe_h = sem("pe_h")
        h_out = sem("h_out")
        h_stored = sem("h_stored")
        staged = sem("staged")
        pool_go = sem("pool_go")
        got = [sem(f"got{j}") for j in range(BODY)]
        s_ready = sem("s_ready")
        p_ready = sem("p_ready")
        late_ready = sem("late_ready")
        x_got = sem("x_got")
        x_s = sem("x_s")
        x_p = sem("x_p")
        x_acc = sem("x_acc")
        acc_done = sem("acc_done")
        pe_z = sem("pe_z")
        z_out = sem("z_out")
        bvar_ready = sem("bvar_ready")
        bsqrt_done = sem("bsqrt_done")
        coef_ready = sem("coef_ready")
        y_out = sem("y_out")
        act_in = sem("act_in")
        res_mul = sem("res_mul")
        pe_back = sem("pe_back")
        x1_ready = sem("x1_ready")
        pe_lgT = sem("pe_lgT")
        lgT_done = sem("lgT_done")
        pe_gate = sem("pe_gate")
        lg_ready = sem("lg_ready")
        exp_done = sem("exp_done")
        hot_ready = sem("hot_ready")
        pe_rank = sem("pe_rank")
        slots_ready = sem("slots_ready")
        x1_stored = sem("x1_stored")
        dispatched = sem("dispatched")
        w1_raw = sem("w1_raw")
        w2_raw = sem("w2_raw")
        be2_in = [sem(f"be2_in{i}") for i in range(2)]
        erow_in = [sem(f"erow_in{i}") for i in range(2)]
        erest_in = [sem(f"erest_in{i}") for i in range(2)]
        w1h_done = sem("w1h_done")
        w1l_done = sem("w1l_done")
        w2h_done = sem("w2h_done")
        w2l_done = sem("w2l_done")
        pads_done = sem("pads_done")
        pe_in = sem("pe_in")
        inh_done = sem("inh_done")
        inl_done = sem("inl_done")
        pe_hid = sem("pe_hid")
        hidf_done = sem("hidf_done")
        hidh_done = sem("hidh_done")
        hidl_done = sem("hidl_done")
        pe_y = sem("pe_y")
        y_read = sem("y_read")
        dve_go = sem("dve_go")
        yv_done = sem("yv_done")
        y_step = sem("y_step")
        mask_done = sem("mask_done")
        y_ready = sem("y_ready")
        y_sent = [sem(f"y_sent{i}") for i in range(ST)]

        def expert_bias(i, k, f):
            return cols[:, bass.ds(i * (2 * FT) + (k * FT + f), 1)]

        B2, G, B, BNG, BNB = range(5)
        VEC = NE * FT

        def vec(l, which, h=None):
            c = VEC + (l * 5 + which) * H
            return cols[:, c:c + H] if h is None else cols[:, c + h:c + h + 1]

        PAIRS = [(2 * j, min(2, TILES - 2 * j)) for j in range(-(-TILES // 2))]
        NP = len(PAIRS)
        EDGES_AT = 3
        WIDTH = [b - a for a, b in zip(START, START[1:])]

        def blocks_to(tile):
            return sum(a < tile * P for a in START[:-1])

        ZEROED = 2 * GROUP
        ACC = ZEROED + CHUNKS

        T_BANKS = ((6, 7), (5, 6, 7))
        H_BANKS = (4, 5, 0, 1)
        BACK_BANKS = (0, 1, 3)
        GBLOCKS = -(-TILES // 4)
        STORES = len(XG) + 1
        xt = x[0:(TILES - 1) * P, :].rearrange("(t p) d -> p t d", p=P)
        w1v = w1.rearrange("e (h p) f -> p (e h) f", p=P)
        w2v = w2.rearrange("e (f p) n -> p (e f) n", p=P)
        ebv = ebuf.rearrange("(t p) r -> p t r", p=P)

        def experts(eng, one):
            one(0, 0, True, False)
            one(0, 1, False, False)
            with eng.Fori(1, NE // 2 - 1, 1) as i:
                for k in range(2):
                    one(i, k, False, False)
            one(NE // 2 - 1, 0, False, False)
            one(NE // 2 - 1, 1, False, True)

        block = ctx.enter_context(nc.Block())

        @block.sync
        def _(sp):
            def load_x(g):
                a, b = XG[g]
                if b == TILES:
                    sp.wait_ge(tail_zero, 1)
                    sp.dma_start(rows[0:TAIL, TILES - 1, D:2 * D], x[(TILES - 1) * P:, :]).then_inc(x_in[g], 16)
                    b -= 1
                sp.dma_start(rows[:, a:b, D:2 * D], xt[:, a:b, :]).then_inc(x_in[g], 16)

            load_x(1)
            whole, rest = CHUNKS - 1 - (GROUPS - 1) * P, E - (CHUNKS - 1) * P
            sp.wait_ge(meta_zero, 4)
            for ap, to in ((src, metaI[:, 0]), (dst, metaI[:, 1]), (ew, metaF[:, 2])):
                g3, cut = (GROUPS - 1) * P * P, (CHUNKS - 1) * P
                sp.dma_start(to[:, 0:GROUPS - 1, :], ap[0:g3].rearrange("(g c e) -> c g e", c=P, e=P)).then_inc(meta_in, 16)
                sp.dma_start(to[0:whole, GROUPS - 1, :], ap[g3:cut].rearrange("(c e) -> c e", e=P)).then_inc(meta_in, 16)
                sp.dma_start(to[whole:whole + 1, GROUPS - 1, 0:rest], ap[cut:E].rearrange("(c e) -> c e", c=1)).then_inc(meta_in, 16)
            for g in range(2, len(XG)):
                load_x(g)

            for l in range(2):
                ht = h_dram[l][0:(TILES - 1) * P, :].rearrange("(t p) d -> p t d", p=P)
                for a, b in XG:
                    sp.wait_ge(h_out, l * NP + -(-b // 2))
                    if b == TILES:
                        b -= 1
                        sp.dma_start(h_dram[l][b * P:, :], rows[0:TAIL, b, 0:D]).then_inc(h_stored, 16)
                    sp.dma_start(ht[:, a:b, :], rows[:, a:b, 0:D]).then_inc(h_stored, 16)
                if l == 0:
                    sp.wait_ge(fill_ready, 2)
                    with sp.Fori(0, NE * ST, 1) as i:
                        sp.wait_ge(acc_done, i * BLOCK + (ZEROED + BLOCK))
                        sp.dma_start(ebuf[bass.ds(i * P, P), :], fill).then_inc(filled, 16)
                    sp.wait_ge(filled, 16 * NE * ST)
                    sp.dma_start(we1[:, :, :], w1v[:, 0:H, :]).then_inc(w1_raw, 16)
                    sp.dma_start(we2[:, :, :], w2v[:, 0:FT, :]).then_inc(w2_raw, 16)
                    sp.dma_start(be2[:, 0, :], b2[0:1, :].partition_broadcast(P)).then_inc(be2_in[0], 16)
            ot = out[0:(TILES - 1) * P, :].rearrange("(t p) d -> p t d", p=P)
            for a, b in XG:
                sp.wait_ge(x1_ready, -(-b // 2))
                if b == TILES:
                    b -= 1
                    sp.dma_start(out[b * P:, :], rows[0:TAIL, b, D:2 * D]).then_inc(x1_stored, 16)
                sp.dma_start(ot[:, a:b, :], rows[:, a:b, D:2 * D]).then_inc(x1_stored, 16)
            sp.wait_ge(dispatched, 16 * TILES)
            sp.wait_ge(x1_stored, 16 * STORES)
            sp.dma_start(erow[0], ebv[:, 0:ST, 0:D]).then_inc(erow_in[0], 16)
            sp.dma_start(erest[0], ebv[:, 0:ST, D:]).then_inc(erest_in[0], 16)

            def next_expert(i, k, first, last):
                if last:
                    return
                if not first:
                    sp.wait_ge(pe_in, i * 2 + k)
                sp.dma_start(erow[1 - k], ebv[:, bass.ds(i * (2 * ST) + (k + 1) * ST, ST), 0:D]).then_inc(erow_in[1 - k], 16)
                sp.wait_ge(w1l_done, i * 2 + (k + 1))
                sp.dma_start(we1[:, :, :], w1v[:, bass.ds(i * (2 * H) + (k + 1) * H, H), :]).then_inc(w1_raw, 16)
                if not first:
                    for s in range(ST):
                        sp.wait_ge(y_sent[s], i * 32 + 16 * k)
                sp.dma_start(erest[1 - k], ebv[:, bass.ds(i * (2 * ST) + (k + 1) * ST, ST), D:]).then_inc(erest_in[1 - k], 16)
                sp.dma_start(be2[:, 1 - k, :], b2[bass.ds(i * 2 + (k + 1), 1), :].partition_broadcast(P)).then_inc(be2_in[1 - k], 16)
                sp.wait_ge(w2l_done, i * 2 + (k + 1))
                sp.dma_start(we2[:, :, :], w2v[:, bass.ds(i * (2 * FT) + (k + 1) * FT, FT), :]).then_inc(w2_raw, 16)

            experts(sp, next_expert)
            for s in range(ST):
                sp.wait_ge(y_sent[s], 16 * NE)

        @block.gpsimd
        def _(pool):
            nc.gpsimd.memset(metaI[:, 0, GROUPS - 1, :], 0).then_inc(meta_zero, 1)
            nc.gpsimd.memset(metaI[:, 1, GROUPS - 1, :], NPAD + P).then_inc(meta_zero, 1)
            nc.gpsimd.memset(metaF[:, 2, GROUPS - 1, :], 0.0).then_inc(meta_zero, 1)
            nc.gpsimd.memset(colsrc, 0.0).then_inc(meta_zero, 1)
            nc.gpsimd.iota(iota_i[:, :], [[1, P]], base=0, channel_multiplier=0).then_inc(consts, 1)
            nc.gpsimd.iota(bound_i[:, :], [[P, CROSS]], base=P, channel_multiplier=0).then_inc(consts, 1)
            nc.gpsimd.iota(rank_i[:, :], [[-1, NE]], base=NE, channel_multiplier=0).then_inc(consts, 1)
            nc.gpsimd.iota(base_i[:, :], [[ESLOT, NE]], base=-1, channel_multiplier=0).then_inc(consts, 1)
            nc.gpsimd.iota(tok_i[:, :], [[P, TILES]], base=0, channel_multiplier=1).then_inc(consts, 1)
            nc.gpsimd.memset(ident[:, :], 0.0).then_inc(consts, 1)
            nc.gpsimd.memset(upper[:, :], 1.0).then_inc(consts, 1)
            nc.gpsimd.memset(ones[:, :], 1.0).then_inc(consts, 1)
            pool.wait_ge(consts, 8)
            nc.gpsimd.affine_select(out=ident[:, :], in_=ident[:, :], compare_op=ALU.not_equal, fill=1.0, base=0,
                                    pattern=[[-1, P]], channel_multiplier=1).then_inc(consts, 1)
            nc.gpsimd.affine_select(out=upper[:, :], in_=upper[:, :], compare_op=ALU.is_ge, fill=0.0, base=0,
                                    pattern=[[1, P]], channel_multiplier=-1).then_inc(consts, 1)
            nc.gpsimd.memset(fill, 0.0).then_inc(fill_ready, 1)
            pool.wait_ge(fill_ready, 1)
            nc.gpsimd.memset(fill[:, 2 * D:2 * D + 1].bitcast(I32), FAR).then_inc(fill_ready, 1)
            nc.gpsimd.memset(metaE[:, :, CHUNKS:], 0.0).then_inc(pads, 1)
            nc.gpsimd.memset(zT[:, :, N:], 0.0).then_inc(pads, 1)

            pool.wait_ge(meta_zero, 4)
            for l in range(2):
                for k in range(2):
                    if l or k:
                        pool.dma_start(wc[:, l, k], conv[l]["w1" if k == 0 else "w2"].rearrange("(h p) n -> p h n", p=P)).then_inc(small_in, 16)
                for k, name in enumerate(("b2", "g", "b", "bng", "bnb")):
                    r = VEC + (l * 5 + k) * H
                    pool.dma_start(colsrc[r:r + H, :], conv[l][name].rearrange("(h p) -> h p", p=P)).then_inc(cols_in, 16)
            pool.dma_start(b1row[:, 1, :], conv[1]["b1"].rearrange("(a n) -> a n", a=1).partition_broadcast(P)).then_inc(small_in, 16)
            pool.dma_start(colsrc[0:NE * FT, :], b1.rearrange("e (f p) -> (e f) p", p=P)).then_inc(cols_in, 16)
            pool.dma_start(gw[:, :, :], gate_w.rearrange("(h p) n -> p h n", p=P)).then_inc(small_in, 16)
            pool.dma_start(gb[:, :], gate_b.rearrange("(n a) -> n a", a=1)).then_inc(small_in, 16)

            late = None
            for l in range(2):
                if l == 0:
                    pool.wait_ge(pe_meta, 1)
                else:
                    pool.wait_ge(pe_z, NB * H)
                nc.gpsimd.memset(aggT[:, :, :], 0.0).then_inc(acc_done, ZEROED)
                pool.wait_ge(h_stored, 16 * STORES * (l + 1))
                with pool.Fori(0, ITER, 1) as i:
                    for b in range(2):
                        pool.wait_ge(staged, i * 2 + (l * (BLOCKS + 1) + b + 1))
                        pool.sem_inc(pool_go, 1)
                        for k in range(BLOCK):
                            nc.gpsimd.indirect_dma_start(
                                out=msgs[:, b * BLOCK + k, :], out_offset=None, in_=h_dram[l],
                                in_offset=bass.IndirectOffsetOnAxis(ap=idx_now[:, b, k:k + 1], axis=0),
                            ).then_inc(got[b * BLOCK + k], 16)
                if late is None:
                    pool.wait_ge(late_ready, 1)
                    late = pool.value_load(late_i[0:1, 0:1], min_val=0, max_val=E + NB)
                with pool.If(late > 0):
                    pool.wait_ge(acc_done, (l + 1) * ACC)
                    for u in range(CROSS):
                        if u >= BODY and u % GROUP == 0:
                            pool.wait_ge(x_acc, l * CROSS + u - BODY + GROUP)
                        nc.gpsimd.indirect_dma_start(
                            out=msgs[:, u % BODY, :], out_offset=None, in_=h_dram[l],
                            in_offset=bass.IndirectOffsetOnAxis(ap=idx_x[:, u:u + 1], axis=0),
                        ).then_inc(x_got, 16)
                        if u % GROUP == GROUP - 1:
                            pool.wait_ge(x_got, 16 * (l * CROSS + u + 1))
            pool.wait_ge(filled, 16 * NE * ST)
            for t in range(TILES):
                for p, (a, b) in enumerate(PARTS):
                    if t == a:
                        pool.wait_ge(slots_ready, p + 1)
                nc.gpsimd.indirect_dma_start(
                    out=ebuf, out_offset=bass.IndirectOffsetOnAxis(ap=slot_i[:, t:t + 1], axis=0),
                    in_=rows[:, t, :], in_offset=None, bounds_check=NE * ESLOT - 1, oob_is_err=False,
                ).then_inc(dispatched, 16)
            pool.wait_ge(x1_stored, 16 * STORES)

            def lows_and_rows(i, k, first, last):
                if not last:
                    pool.wait_ge(w1h_done, i * 2 + (k + 2))
                    nc.gpsimd.tensor_tensor(w1l[:, :, :], we1[:, :, :], w1h[:, :, :].bitcast(F32), ALU.subtract).then_inc(w1l_done, 1)
                for p in range(2):
                    pool.wait_ge(yv_done, i * 4 + (2 * k + p + 1))
                    nc.gpsimd.tensor_tensor(ymask, yv, yv, ALU.subtract).then_inc(mask_done, 1)
                    if p and not last:
                        pool.wait_ge(w2h_done, i * 2 + (k + 2))
                        nc.gpsimd.tensor_tensor(w2l[:, :, :], we2[:, :, :], w2h[:, :, :].bitcast(F32), ALU.subtract).then_inc(w2l_done, 1)
                    pool.wait_ge(y_ready, i * 4 + (2 * k + p + 1))
                    pool.sem_inc(pool_go, 1)
                    for s in range(2 * p, 2 * p + 2):
                        nc.gpsimd.indirect_dma_start(
                            out=out, out_offset=bass.IndirectOffsetOnAxis(ap=erest[k][:, s, D:D + 1].bitcast(I32), axis=0),
                            in_=yo[:, s, :], in_offset=None, bounds_check=N - 1, oob_is_err=False,
                        ).then_inc(y_sent[s], 16)

            experts(pool, lows_and_rows)

        @block.tensor
        def _(pe):
            pe.wait_ge(consts, 10)

            def rows_to_T(n, j):
                t, w = PAIRS[j]
                if n and t >= XG[3][0]:
                    pe.wait_ge(rows_norm_v, t + w - XG[3][0])
                else:
                    pe.wait_ge(rows_norm, n * TILES + t + w)
                B = T_BANKS[n]
                if j >= len(B):
                    pe.wait_ge(tr_out, n * NP + j + 1 - len(B))
                for h in range(H):
                    for k in range(w):
                        mm = nc.tensor.transpose(bank[B[j % len(B)]][:, h * 256 + k * P:h * 256 + (k + 1) * P],
                                                 rows[:, t + k, h * P:(h + 1) * P], ident[:, :])
                mm.then_inc(pe_tr, 1)

            def h_rows(l, j):
                t, w = PAIRS[j]
                if l == 0:
                    pe.wait_ge(tr_out, j + 1)
                else:
                    pe.wait_ge(act_in, blocks_to(t + w) * H)
                if l == 0 and j == 2:
                    pe.wait_ge(metaE_done, 3)
                if j >= len(H_BANKS):
                    pe.wait_ge(h_sum, l * NP + j + 1 - len(H_BANKS))
                for k in range(w):
                    o = bank[H_BANKS[j % 4]][:, k * D:(k + 1) * D]
                    for h in range(H):
                        mm = nc.tensor.matmul(o, (xnT, zT)[l][:, h, (t + k) * P:(t + k + 1) * P], wc[:, l, 0, h, :], start=(h == 0), stop=(h == H - 1))
                mm.then_inc(pe_h, 1)

            def z_blocks(first, end):
                for n in range(first * H, end * H):
                    j, fo = divmod(n, H)
                    if n >= 4:
                        pe.wait_ge(z_out, l * NB * H + n - 3)
                    for h in range(H):
                        mm = nc.tensor.matmul(bank[4 + n % 4][:, 0:WIDTH[j]], wc[:, l, 1, h, fo * P:(fo + 1) * P],
                                              aggT[:, h, START[j]:START[j + 1]], start=(h == 0), stop=(h == H - 1))
                    mm.then_inc(pe_z, 1)

            def edges_to_partitions():
                pe.wait_ge(meta_rel, 1)
                for k in range(3):
                    for g in range(GROUPS):
                        a = relT[:, g, :] if k == 1 else metaF[:, k, g, :]
                        mm = nc.tensor.transpose(bank[k][:, g * P:(g + 1) * P], a, ident[:, :])
                mm.then_inc(p_ready, 1)
                for k in range(3):
                    for g in range(GROUPS):
                        a = farW[:, g, :] if k == 2 else metaF[:, k, g, :]
                        nc.tensor.matmul(bank[3][:, k * 32:k * 32 + CROSS], a, pick[:, g, :], start=(g == 0), stop=(g == GROUPS - 1))
                for g in range(GROUPS):
                    nc.tensor.matmul(bank[3][0:1, 24:25], nfar[:, g:g + 1], ones[:, 0:1], start=(g == 0), stop=(g == GROUPS - 1))
                for g in range(GROUPS):
                    mm = nc.tensor.matmul(bank[3][0:1, 96 + g * P:min(96 + (g + 1) * P, 512)], metaF[:, 1, g, 0:1],
                                          ident[:, 0:min(P, CHUNKS - g * P)], start=True, stop=True)
                mm.then_inc(pe_meta, 1)

            for j in range(NP + 2):
                if j == EDGES_AT:
                    edges_to_partitions()
                if j < NP:
                    rows_to_T(0, j)
                if j == 2:
                    pe.wait_ge(w1_in, 32)
                if j >= 2:
                    h_rows(0, j - 2)
            pe.wait_ge(tr_out, NP)
            pe.wait_ge(cols_in, 16 * 11)
            nc.tensor.transpose(bank[6][:, 0:P], colsrc, ident[:, :]).then_inc(pe_cols, 1)
            pe.wait_ge(small_in, 16 * 6)
            pe.wait_ge(late_ready, 1)
            late = pe.value_load(late_i[0:1, 0:1], min_val=0, max_val=E + NB)
            for l in range(2):
                if l:
                    for j in range(NP):
                        h_rows(1, j)
                for n, (a, b) in enumerate(zip([0] + EARLY, EARLY + [ITER])):
                    with pe.Fori(a, b, 1) as i:
                        for q in range(4):
                            pe.wait_ge(s_ready, i * 4 + (l * (NGROUP + 1) + q + 1))
                            pe.wait_ge(acc_done, i * (4 * GROUP) + (l * ACC + (q + 1) * GROUP))
                            for k in range(GROUP):
                                j = q * GROUP + k
                                pe.wait_ge(got[j], i * 16 + 16 * (l * ITER + 1))
                                o = bank[2 * (q % 2) + k // 2]
                                for h in range(H):
                                    mm = nc.tensor.matmul(o[:, (k % 2) * 256 + h * P:(k % 2) * 256 + (h + 1) * P],
                                                          msgs[:, j, h * P:(h + 1) * P], S[:, (q % 2) * GROUP + k, :],
                                                          start=True, stop=True)
                            mm.then_inc(p_ready, 1)
                    if b < ITER:
                        with pe.If(late == 0):
                            pe.wait_ge(acc_done, l * ACC + ZEROED + b * BODY - GROUP)
                            z_blocks(n, n + 1)
                pe.wait_ge(acc_done, (l + 1) * ACC)
                with pe.If(late > 0):
                    for g in range(XGROUP):
                        pe.wait_ge(x_s, l * XGROUP + g + 1)
                        pe.wait_ge(x_got, 16 * (l * CROSS + (g + 1) * GROUP))
                        if g:
                            pe.wait_ge(x_acc, l * CROSS + g * GROUP)
                        for k in range(GROUP):
                            u = g * GROUP + k
                            for h in range(H):
                                mm = nc.tensor.matmul(bank[k // 2][:, (k % 2) * 256 + h * P:(k % 2) * 256 + (h + 1) * P],
                                                      msgs[:, u % BODY, h * P:(h + 1) * P], S[:, k, :], start=True, stop=True)
                        mm.then_inc(x_p, 1)
                    pe.wait_ge(x_acc, (l + 1) * CROSS)
                    z_blocks(0, len(EARLY))
                z_blocks(len(EARLY), NB)
                pe.wait_ge(z_out, (l + 1) * NB * H)
            for j, (t, w) in enumerate(PAIRS):
                pe.wait_ge(act_in, (NB + blocks_to(t + w)) * H)
                if j >= 3:
                    pe.wait_ge(x1_ready, j - 2)
                for k in range(w):
                    for h in range(H):
                        mm = nc.tensor.transpose(bank[BACK_BANKS[j % 3]][:, k * D + h * P:k * D + (h + 1) * P],
                                                 zT[:, h, (t + k) * P:(t + k + 1) * P], ident[:, :])
                mm.then_inc(pe_back, 1)
            def rank_part(p):
                hots = gate_tables[p][2].rearrange("p e t -> p (e t)")
                n = hots.shape[1]
                pe.wait_ge(hot_ready, p + 1)
                nc.tensor.matmul(bank[0][:, 0:n], upper[:, :], hots, start=True, stop=True)
                nc.tensor.matmul(bank[1][:, 0:n], ones[:, :], hots, start=True, stop=True).then_inc(pe_rank, 1)

            def logits(b):
                t0, t1 = 4 * b, min(4 * b + 4, TILES)
                pe.wait_ge(tr_out, NP + t1 // 2 + t1 % 2)
                if b:
                    pe.wait_ge(lgT_done, b)
                for h in range(H):
                    mm = nc.tensor.matmul(bank[4][0:NE, 0:(t1 - t0) * P], gw[:, h, :], aggT[:, h, t0 * P:t1 * P],
                                          start=(h == 0), stop=(h == H - 1))
                mm.then_inc(pe_lgT, 1)

            def logits_back(b):
                pe.wait_ge(lgT_done, b + 1)
                if 4 * b == SPLIT:
                    pe.wait_ge(x1_ready, NP)
                for t in range(4 * b, min(4 * b + 4, TILES)):
                    mm = nc.tensor.transpose(bank[2 + (t >= SPLIT)][:, t * NE:(t + 1) * NE], lgT[:, t * P:(t + 1) * P], ident[0:NE, 0:NE])
                if t + 1 in (SPLIT, TILES):
                    mm.then_inc(pe_gate, 1)

            for j in range(2 * GBLOCKS + 3):
                if j < NP:
                    rows_to_T(1, j)
                if j == 2 * (SPLIT // 4) + 4:
                    rank_part(0)
                b, odd = divmod(j - 3, 2)
                if odd:
                    if 0 <= b < GBLOCKS:
                        logits_back(b)
                elif 0 <= b < GBLOCKS:
                    logits(b)
            rank_part(1)

            def expert_in(k, loads):
                pe.wait_ge(erow_in[k], loads)
                for h in range(H):
                    for s in range(ST):
                        mm = nc.tensor.transpose(bank[h][:, s * P:(s + 1) * P], erow[k][:, s, h * P:(h + 1) * P], ident[:, :])
                mm.then_inc(pe_in, 1)

            def expert(i, k, first, last):
                pe.wait_ge(inl_done, i * (2 * H) + (k + 1) * H)
                pe.wait_ge(w1l_done, i * 2 + (k + 1))
                for f in range(FT):
                    if not first or f >= 4:
                        pe.wait_ge(hidf_done, i * (2 * FT) + (k * FT + f - 3))
                    n = 0
                    for h in range(H):
                        for a, b in ((w1h, inh), (w1l, inh), (w1h, inl)):
                            mm = nc.tensor.matmul(bank[2 + f % 4][:, 0:USED], a[:, h, f * P:(f + 1) * P], b[:, h, :],
                                                  start=(n == 0), stop=(n == 3 * H - 1))
                            n += 1
                    mm.then_inc(pe_hid, 1)
                if not last:
                    expert_in(1 - k, i * 16 + 16 * (k + 1))
                pe.wait_ge(w2l_done, i * 2 + (k + 1))
                for s in range(ST):
                    if s % 2 == 0 and not first:
                        pe.wait_ge(y_read, i * 4 + (2 * k + s // 2 - 1))
                    n = 0
                    for f in range(FT):
                        if s == 0:
                            pe.wait_ge(hidl_done, i * (2 * FT) + (k * FT + f + 1))
                        for a, b in ((hidh, w2h), (hidl, w2h), (hidh, w2l)):
                            mm = nc.tensor.matmul(bank[6 + s // 2][:, (s % 2) * D:(s % 2 + 1) * D], a[:, f, s * P:(s + 1) * P], b[:, f, :],
                                                  start=(n == 0), stop=(n == 3 * FT - 1))
                            n += 1
                    if s % 2:
                        mm.then_inc(pe_y, 1)

            expert_in(0, 16)
            pe.wait_ge(pads_done, 2 * FT)
            experts(pe, expert)

        @block.scalar
        def _(act):
            def layernorm_sqrt(n, g):
                a, b = XG[g]
                act.wait_ge(var_ready, n * len(XG) + g + 1)
                nc.scalar.activation(sq[:, a:b], sd[:, a:b], ACT.Sqrt).then_inc(sqrt_done, 1)

            def T_out(n, to, j):
                t, w = PAIRS[j]
                act.wait_ge(pe_tr, n * NP + j + 1)
                nc.scalar.copy(to[:, :, t * P:(t + w) * P],
                               bank[T_BANKS[n][j % len(T_BANKS[n])]][:, :].rearrange("p (h n) -> p h n", h=H)[:, :, 0:w * P]).then_inc(tr_out, 1)

            def h_rows_out(l, j):
                t, w = PAIRS[j]
                act.wait_ge(h_sum, l * NP + j + 1)
                nc.scalar.activation(rows[:, t:t + w, 0:D], rows[:, t:t + w, 0:D], ACT.Relu).then_inc(h_out, 1)

            def z_out_blocks(first, end):
                for n in range(first * H, end * H):
                    j, fo = divmod(n, H)
                    act.wait_ge(pe_z, l * NB * H + n + 1)
                    nc.scalar.activation(zT[:, fo, START[j]:START[j + 1]], bank[4 + n % 4][:, 0:WIDTH[j]], ACT.Identity,
                                         bias=vec(l, B2, fo)).then_inc(z_out, 1)

            def norm_pairs(n, each, groups):
                layernorm_sqrt(n, 0)
                for g, (a, b) in enumerate(XG[:groups]):
                    act.wait_ge(norm_coef, n * len(XG) + g + 1)
                    for j in range(a // 2, -(-b // 2)):
                        if j == -(-b // 2) - 1:
                            for k in range(g + 1, g + 2 if g + 1 < groups else len(XG)):
                                layernorm_sqrt(n, k)
                        for t in range(2 * j, min(2 * j + 2, b)):
                            nc.scalar.activation(rows[:, t, 0:D], rows[:, t, D:2 * D], ACT.Identity, bias=nmr[:, t:t + 1],
                                                 scale=rs[:, t:t + 1]).then_inc(rows_norm, 1)
                        each(j)

            def stage(b, c0):
                nc.scalar.copy(idx_now[:, b, :], metaE[:, 0, bass.ds(c0, BLOCK)])
                nc.scalar.copy(relw_now[:, b, :, :], metaE[:, 1:3, bass.ds(c0, BLOCK)]).then_inc(staged, 1)

            act.dma_start(rows[:, 0:XG[0][1], D:2 * D], xt[:, 0:XG[0][1], :]).then_inc(x_in[0], 16)
            act.dma_start(wc[:, 0, 0], conv[0]["w1"].rearrange("(h p) n -> p h n", p=P)).then_inc(w1_in, 16)
            act.dma_start(b1row[:, 0, :], conv[0]["b1"].rearrange("(a n) -> a n", a=1).partition_broadcast(P)).then_inc(w1_in, 16)

            def first_pair(j):
                if j == 0:
                    act.wait_ge(meta_in, 16 * 9)
                    nc.scalar.copy(metaF[:, 0:2], metaI[:, :]).then_inc(meta_f, 1)
                if j == EDGES_AT + 1:
                    act.wait_ge(pe_meta, 1)
                    act.wait_ge(pads, 2)
                    for k in range(3):
                        nc.scalar.copy(metaE[:, k, 0:CHUNKS], bank[k][:, 0:CHUNKS]).then_inc(metaE_done, 1)
                if j >= 2:
                    T_out(0, xnT, j - 2)
                if j >= 4:
                    h_rows_out(0, j - 4)

            norm_pairs(0, first_pair, len(XG))
            for j in range(NP, NP + 4):
                if j < NP + 2:
                    T_out(0, xnT, j - 2)
                h_rows_out(0, j - 4)
            act.wait_ge(pe_cols, 1)
            nc.scalar.copy(cols[:, :], bank[6][:, 0:P]).then_inc(cols_done, 1)
            act.wait_ge(late_ready, 1)
            late = act.value_load(late_i[0:1, 0:1], min_val=0, max_val=E + NB)
            for l in range(2):
                if l:
                    for j in range(NP):
                        h_rows_out(1, j)
                act.wait_ge(metaE_done, 4)
                stage(0, 0)
                stage(1, BLOCK)
                ends = [e + 1 for e in EARLY]
                for n, (a, b) in enumerate(zip([0] + ends, ends)):
                    with act.Fori(a, b, 1) as i:
                        for k in range(2):
                            act.wait_ge(acc_done, i * BODY + (l * ACC + ZEROED + (k + 1) * BLOCK))
                            stage(k, i * BODY + (k + 2) * BLOCK)
                    with act.If(late == 0):
                        z_out_blocks(n, n + 1)
                act.wait_ge(acc_done, l * ACC + ZEROED + (BLOCKS - 1) * BLOCK)
                stage(0, CHUNKS)
                with act.If(late > 0):
                    z_out_blocks(0, len(EARLY))
                z_out_blocks(len(EARLY), NB)
                for k in range(2):
                    act.wait_ge(bvar_ready, 2 * l + k + 1)
                    nc.scalar.activation(bsq[:, :], bsd[:, :], ACT.Sqrt).then_inc(bsqrt_done, 1)
                    act.wait_ge(coef_ready, 2 * l + k + 1)
                    for n in range(NB * H):
                        j, fo = divmod(n, H)
                        a = zT[:, fo, START[j]:START[j + 1]]
                        if k == 0:
                            nc.scalar.activation(a, a, ACT.Relu, bias=bof[:, fo:fo + 1], scale=bsc[:, fo:fo + 1]).then_inc(y_out, 1)
                        elif l == 0:
                            nc.scalar.activation(a, a, ACT.Relu, bias=bof[:, fo:fo + 1], scale=bsc[:, fo:fo + 1]).then_inc(act_in, 1)
                        else:
                            act.wait_ge(res_mul, n + 1)
                            nc.scalar.activation(a, a, ACT.Relu, bias=bof[:, fo:fo + 1]).then_inc(act_in, 1)
            act.wait_ge(h_stored, 16 * STORES * 2)

            def exp_part(p):
                act.wait_ge(lg_ready, p + 1)
                nc.scalar.activation(gate_tables[p][1], gate_tables[p][0], ACT.Exp).then_inc(exp_done, 1)

            def second_pair(j):
                if j >= 2:
                    T_out(1, aggT, j - 2)
                if j == 4:
                    act.wait_ge(pe_lgT, 1)
                    nc.scalar.activation(lgT[:, 0:512], bank[4][0:NE, :], ACT.Identity, bias=gb[:, 0:1]).then_inc(lgT_done, 1)

            norm_pairs(1, second_pair, 3)
            for j in range(XG[3][0] // 2, NP + 2):
                T_out(1, aggT, j - 2)
                if j == 2 * (SPLIT // 4) + 3:
                    exp_part(0)
            exp_part(1)
            act.wait_ge(slots_ready, 2)
            act.wait_ge(w1_raw, 16)
            nc.scalar.copy(w1h[:, :, :], we1[:, :, :]).then_inc(w1h_done, 1)
            act.wait_ge(w2_raw, 16)
            nc.scalar.copy(w2h[:, :, :], we2[:, :, :]).then_inc(w2h_done, 1)

            def in_high(count):
                act.wait_ge(pe_in, count)
                for h in range(H):
                    nc.scalar.copy(inh[:, h, :], bank[h][:, 0:USED]).then_inc(inh_done, 1)

            in_high(1)

            def highs(i, k, first, last):
                if not first:
                    act.wait_ge(w2_raw, i * 32 + 16 * (k + 1))
                    act.wait_ge(pe_y, i * 4 + 2 * k)
                    nc.scalar.copy(w2h[:, :, :], we2[:, :, :]).then_inc(w2h_done, 1)
                for f in range(FT):
                    act.wait_ge(pe_hid, i * (2 * FT) + (k * FT + f + 1))
                    if not first or f >= 4:
                        act.wait_ge(hidl_done, i * (2 * FT) + (k * FT + f - 3))
                    nc.scalar.activation(hidf[:, f % 4, :], bank[2 + f % 4][:, 0:USED], ACT.Relu,
                                         bias=expert_bias(i, k, f)).then_inc(hidf_done, 1)
                    act.wait_ge(hidf_done, i * (2 * FT) + (k * FT + f + 1))
                    nc.scalar.copy(hidh[:, f, 0:USED], hidf[:, f % 4, :]).then_inc(hidh_done, 1)
                if not last:
                    act.wait_ge(w1_raw, i * 32 + 16 * (k + 2))
                    nc.scalar.copy(w1h[:, :, :], we1[:, :, :]).then_inc(w1h_done, 1)
                    in_high(i * 2 + (k + 2))

            experts(act, highs)

        @block.vector
        def _(dve):
            chain = [0]

            def then(ins):
                chain[0] += 1
                ins.then_inc(dve_chain, 1)
                dve.wait_ge(dve_chain, chain[0])

            def layernorm(n, g, arrived):
                a, b = XG[g]
                for t in range(a, b):
                    arrived(t)
                    c = nc.vector.bn_stats(st[:, t, :], rows[:, t, D:2 * D])
                then(c)
                for t in range(a, b):
                    c = nc.vector.bn_aggr(mv[:, t, :], st[:, t, :])
                then(c)
                nc.vector.tensor_scalar(sd[:, a:b], mv[:, a:b, 1], EPS, None, ALU.add).then_inc(var_ready, 1)

            def layernorm_coef(n, g):
                a, b = XG[g]
                dve.wait_ge(sqrt_done, n * len(XG) + g + 1)
                then(nc.vector.reciprocal(rs[:, a:b], sq[:, a:b]))
                nc.vector.scalar_tensor_tensor(out=nmr[:, a:b], in0=mv[:, a:b, 0], scalar=-1.0, in1=rs[:, a:b],
                                               op0=ALU.mult, op1=ALU.mult).then_inc(norm_coef, 1)

            def h_plus_bias(l, j):
                t, w = PAIRS[j]
                dve.wait_ge(pe_h, l * NP + j + 1)
                nc.vector.tensor_tensor(rows[:, t:t + w, 0:D], bank[H_BANKS[j % 4]][:, 0:w * D].rearrange("p (t d) -> p t d", t=w),
                                        b1row[:, l:l + 1, :].broadcast_to([P, w, D]), ALU.add).then_inc(h_sum, 1)

            nc.vector.memset(rows[:, TILES - 1, D:2 * D], 0.0).then_inc(tail_zero, 1)

            def edges_prepared():
                dve.wait_ge(consts, 10)
                nc.vector.tensor_copy(iota_f[:, :], iota_i[:, :])
                nc.vector.tensor_copy(rank[:, :], rank_i[:, :])
                nc.vector.tensor_copy(base[:, :], base_i[:, :])
                nc.vector.tensor_copy(tok_f[:, :], tok_i[:, :])
                nc.vector.tensor_copy(rows[:, :, 2 * D].bitcast(I32), tok_i[:, :])
                for k in (keep, keep1):
                    nc.vector.memset(k[:, :, :], 1.0)
                then(nc.vector.tensor_copy(bound[:, :], bound_i[:, :]))
                for k in (keep, keep1):
                    nc.vector.memset(k[:, :, 0], 0.0)
                nc.vector.tensor_scalar(invalid[:, :], tok_f[:, :], float(N), float(FAR), ALU.is_ge, ALU.mult)
                nc.vector.tensor_scalar(valid[:, :], tok_f[:, TILES - 1:], float(N), None, ALU.is_lt)
                dve.wait_ge(meta_f, 1)
                for g in range(GROUPS):
                    nc.vector.tensor_scalar(gt_first[:, g, :], bound[:, :], metaF[:, 1, g, 0:1], None, ALU.is_gt)
                    c = nc.vector.tensor_scalar(relT[:, g, :], metaF[:, 1, g, :], metaF[:, 1, g, 0:1], None, ALU.subtract)
                then(c)
                for g in range(GROUPS):
                    nc.vector.scalar_tensor_tensor(out=pick[:, g, :], in0=bound[:, :], scalar=metaF[:, 1, g, P - 1:P],
                                                   in1=gt_first[:, g, :], op0=ALU.is_le, op1=ALU.mult)
                nc.vector.tensor_scalar(farW, metaF[:, 2], 0.0, None, ALU.not_equal)
                then(nc.vector.tensor_scalar(far, relT, float(P), None, ALU.is_ge))
                then(nc.vector.tensor_tensor(farW, farW, far, ALU.mult))
                then(nc.vector.tensor_reduce(nfar[:, :], farW, AX_X, ALU.add))
                nc.vector.tensor_tensor(farW, metaF[:, 2], far, ALU.mult).then_inc(meta_rel, 1)

            def edges_placed():
                dve.wait_ge(pe_meta, 1)
                nc.vector.tensor_copy(idx_x[:, :], bank[3][:, 0:CROSS])
                nc.vector.tensor_tensor(metaX[:, 1, :], bank[3][:, 32:32 + CROSS], bound[:, :], ALU.subtract)
                nc.vector.tensor_copy(metaX[:, 2, :], bank[3][:, 64:64 + CROSS])
                nc.vector.tensor_copy(late_f[:, NB:], bank[3][0:1, 24:25])
                nc.vector.tensor_copy(offs[:, :], bank[3][0:1, 96:96 + CHUNKS])
                nc.vector.tensor_copy(offs_f[:, :], bank[3][0:1, 96:96 + CHUNKS]).then_inc(metaE_done, 1)

            def x_arrived(t):
                g = next(g for g, (a, b) in enumerate(XG) if a <= t < b)
                if XG[g][0] == t:
                    dve.wait_ge(x_in[g], 32 if XG[g][1] == TILES else 16)

            dve.wait_ge(consts, 10)
            adds = {3: range(1, 3), 4: range(3, 6)}
            for g in range(len(XG)):
                layernorm(0, g, x_arrived)
                for j in adds.get(g, ()):
                    h_plus_bias(0, j)
                layernorm_coef(0, g)
                if g == 1:
                    edges_prepared()
                elif g == 2:
                    h_plus_bias(0, 0)
            for j in range(6, NP):
                h_plus_bias(0, j)
                if j == 6:
                    edges_placed()
            dve.wait_ge(metaE_done, 4)
            nc.vector.memset(late_f[:, len(EARLY):NB], 0.0)
            for j, i in enumerate(EARLY):
                c = nc.vector.tensor_scalar(late_f[:, j:j + 1], offs_f[:, i * BODY - GROUP:i * BODY - GROUP + 1], float(START[j + 1]), None, ALU.is_lt)
            then(c)
            then(nc.vector.tensor_reduce(late_f[:, 0:1], late_f[:, :], AX_X, ALU.add))
            nc.vector.tensor_copy(late_i[:, :], late_f[:, 0:1]).then_inc(late_ready, 1)
            dve.wait_ge(late_ready, 1)
            late = dve.value_load(late_i[0:1, 0:1], min_val=0, max_val=E + NB)

            def build_S(half, q):
                b, c0 = (q // 2) % 2, (q % 2) * GROUP
                for k in range(GROUP):
                    c = nc.vector.tensor_scalar(S[:, half * GROUP + k, :], iota_f[:, :], relw_now[:, b, 0, c0 + k:c0 + k + 1],
                                                relw_now[:, b, 1, c0 + k:c0 + k + 1], ALU.is_equal, ALU.mult)
                c.then_inc(s_ready, 1)

            def stats(n):
                j, fo = divmod(n, H)
                return nc.vector.bn_stats(bst[:, fo, j, :], zT[:, fo, START[j]:START[j + 1]])

            def z_stats(n):
                dve.wait_ge(z_out, l * NB * H + n + 1)
                return stats(n)

            for l in range(2):
                if l:
                    for j in range(NP):
                        h_plus_bias(1, j)
                else:
                    dve.wait_ge(cols_done, 1)
                dve.wait_ge(staged, l * (BLOCKS + 1) + 1)
                build_S(0, 0)
                ends = [e + 2 for e in EARLY]
                assert ends[-1] == ITER
                for n, (a, b) in enumerate(zip([0] + ends, ends)):
                    with dve.Fori(a, b, 1) as i:
                        for q in range(4):
                            dve.wait_ge(p_ready, i * 4 + (l * NGROUP + q + 1))
                            if q % 2:
                                dve.wait_ge(staged, i * 2 + (l * (BLOCKS + 1) + (q + 1) // 2 + 1))
                            build_S((q + 1) % 2, q + 1)
                            _, at = nc.values_load_multi_w_load_instructions(
                                offs[0:1, bass.ds(i * BODY + q * GROUP, GROUP)], engines=[mybir.EngineType.DVE],
                                min_val=0, max_val=N - 1, skip_runtime_bounds_check_because="dst lies in [0, N)")
                            dve.wait_ge(p_ready, i * 4 + (l * NGROUP + q + 2))
                            for k in range(GROUP):
                                dve.wait_ge(acc_done, i * BODY + (l * ACC + ZEROED + q * GROUP + k))
                                a = aggT[:, :, bass.ds(at[k], P)]
                                o = bank[2 * (q % 2) + k // 2][:, (k % 2) * 256:(k % 2 + 1) * 256].rearrange("p (h n) -> p h n", h=H)
                                nc.vector.tensor_tensor(a, a, o, ALU.add).then_inc(acc_done, 1)
                    with dve.If(late == 0):
                        for k in range(n * H, (n + 1) * H):
                            z_stats(k)
                with dve.If(late > 0):
                    dve.wait_ge(acc_done, (l + 1) * ACC)
                    for g in range(XGROUP):
                        if g:
                            dve.wait_ge(x_p, l * XGROUP + g)
                        for k in range(GROUP):
                            u = g * GROUP + k
                            c = nc.vector.tensor_scalar(S[:, k, :], iota_f[:, :], metaX[:, 1, u:u + 1], metaX[:, 2, u:u + 1],
                                                        ALU.is_equal, ALU.mult)
                        c.then_inc(x_s, 1)
                        dve.wait_ge(x_p, l * XGROUP + g + 1)
                        for k in range(GROUP):
                            u = g * GROUP + k
                            a = aggT[:, :, (u + 1) * P:(u + 2) * P]
                            o = bank[k // 2][:, (k % 2) * 256:(k % 2 + 1) * 256].rearrange("p (h n) -> p h n", h=H)
                            nc.vector.tensor_tensor(a, a, o, ALU.add).then_inc(x_acc, 1)
                    for n in range(len(EARLY) * H):
                        z_stats(n)

                for k in range(2):
                    for n in range(0 if k else len(EARLY) * H, NB * H):
                        if k:
                            dve.wait_ge(y_out, l * NB * H + n + 1)
                            c = stats(n)
                        else:
                            c = z_stats(n)
                    then(c)
                    for fo in range(H):
                        c = nc.vector.bn_aggr(bmv[:, fo, :], bst[:, fo, :, :].rearrange("p j s -> p (j s)"))
                    then(c)
                    nc.vector.tensor_scalar(bsd[:, :], bmv[:, :, 1], EPS, None, ALU.add).then_inc(bvar_ready, 1)
                    dve.wait_ge(bsqrt_done, 2 * l + k + 1)
                    then(nc.vector.reciprocal(brs[:, :], bsq[:, :]))
                    then(nc.vector.tensor_tensor(bsc[:, :], brs[:, :], vec(l, (G, BNG)[k]), ALU.mult))
                    then(nc.vector.tensor_tensor(bms[:, :], bmv[:, :, 0], bsc[:, :], ALU.mult))
                    nc.vector.tensor_tensor(bof[:, :], vec(l, (B, BNB)[k]), bms[:, :], ALU.subtract).then_inc(coef_ready, 1)
            dve.wait_ge(coef_ready, 4)
            for n in range(NB * H):
                j, fo = divmod(n, H)
                a = zT[:, fo, START[j]:START[j + 1]]
                nc.vector.scalar_tensor_tensor(out=a, in0=a, scalar=bsc[:, fo:fo + 1], in1=xnT[:, fo, START[j]:START[j + 1]],
                                               op0=ALU.mult, op1=ALU.add).then_inc(res_mul, 1)
            done = 0
            for g, (a, b) in enumerate(XG):
                for j in range(done, -(-b // 2)):
                    t, w = PAIRS[j]
                    dve.wait_ge(pe_back, j + 1)
                    nc.vector.tensor_tensor(rows[:, t:t + w, D:2 * D], rows[:, t:t + w, D:2 * D],
                                            bank[BACK_BANKS[j % 3]][:, 0:w * D].rearrange("p (t d) -> p t d", t=w), ALU.add).then_inc(x1_ready, 1)
                done = -(-b // 2)
                if 0 < g < 4:
                    layernorm_coef(1, g - 1)
                layernorm(1, g, lambda t: dve.wait_ge(x1_ready, t // 2 + 1))

            def lgT_out(b):
                w = min(512, NPAD - 512 * b)
                dve.wait_ge(pe_lgT, b + 1)
                nc.vector.tensor_scalar(lgT[:, 512 * b:512 * b + w], bank[4][0:NE, 0:w], gb[:, 0:1], None, ALU.add).then_inc(lgT_done, 1)

            lgT_out(1)
            for g in range(3, len(XG)):
                layernorm_coef(1, g)
                a, b = XG[g]
                dve.wait_ge(norm_coef, len(XG) + g + 1)
                for t in range(a, b):
                    nc.vector.tensor_scalar(rows[:, t, 0:D], rows[:, t, D:2 * D], rs[:, t:t + 1], nmr[:, t:t + 1],
                                            ALU.mult, ALU.add).then_inc(rows_norm_v, 1)

            def wide(v, a, b):
                return v[:, a:b].rearrange("p (o t) -> p o t", o=1).broadcast_to([P, NE, b - a])

            def each(v, n):
                return v[:, :].rearrange("p (e o) -> p e o", o=1).broadcast_to([P, NE, n])

            def by_token(table):
                return table.rearrange("p e t -> p t e")

            def choose(p):
                a, b = PARTS[p]
                n = b - a
                lg, ex, hot, hb, _, _ = gate_tables[p]
                logits = bank[2 + p][:, a * NE:b * NE].rearrange("p (t e) -> p e t", e=NE)
                dve.wait_ge(pe_gate, p + 1)
                then(nc.vector.tensor_reduce(r1[:, a:b], by_token(logits), AX_X, ALU.max))
                nc.vector.tensor_tensor(lg, logits, wide(r1, a, b), ALU.subtract).then_inc(lg_ready, 1)
                dve.wait_ge(exp_done, p + 1)
                nc.vector.tensor_reduce(r2[:, a:b], by_token(ex), AX_X, ALU.add)
                then(nc.vector.tensor_reduce(r1[:, a:b], by_token(ex), AX_X, ALU.max))
                nc.vector.reciprocal(r3[:, a:b], r2[:, a:b])
                then(nc.vector.tensor_tensor(hot, ex, wide(r1, a, b), ALU.is_equal))
                nc.vector.tensor_tensor(rows[:, a:b, 2 * D + 1], r1[:, a:b], r3[:, a:b], ALU.mult)
                then(nc.vector.tensor_tensor(hot, hot, each(rank, n), ALU.mult))
                then(nc.vector.tensor_reduce(r4[:, a:b], by_token(hot), AX_X, ALU.max))
                c = nc.vector.tensor_tensor(hot, hot, wide(r4, a, b), ALU.is_equal)
                if b == TILES:
                    then(c)
                    c = nc.vector.tensor_scalar(hot[:, :, n - 1], hot[:, :, n - 1], valid[:, 0:1], None, ALU.mult)
                c.then_inc(hot_ready, 1)
                dve.wait_ge(hot_ready, p + 1)
                then(nc.vector.tensor_tensor(hb, hot, each(base, n), ALU.mult))
                then(nc.vector.tensor_reduce(r2[:, a:b], by_token(hb), AX_X, ALU.add))
                nc.vector.tensor_tensor(r2[:, a:b], r2[:, a:b], invalid[:, a:b], ALU.add)

            def slots(p):
                a, b = PARTS[p]
                n = b - a
                _, _, hot, _, upto, cum = gate_tables[p]
                in_tile, whole = (bank[k][:, 0:NE * n].rearrange("p (e t) -> p e t", e=NE) for k in range(2))
                flat2 = upto.rearrange("p e t -> p (e t)")
                dve.wait_ge(pe_rank, p + 1)
                nc.vector.tensor_copy(cum, in_tile)
                then(nc.vector.tensor_tensor_scan(flat2, keeps[p], bank[1][:, 0:NE * n], 0.0, ALU.mult, ALU.add))
                c = nc.vector.tensor_tensor(cum, cum, upto, ALU.add)
                if p == 0:
                    nc.vector.tensor_copy(carry[:, :], upto[:, :, n - 1])
                else:
                    then(c)
                    c = nc.vector.tensor_tensor(cum, cum, each(carry, n), ALU.add)
                then(c)
                then(nc.vector.tensor_tensor(cum, cum, whole, ALU.subtract))
                then(nc.vector.tensor_tensor(cum, cum, hot, ALU.mult))
                then(nc.vector.tensor_reduce(r1[:, a:b], by_token(cum), AX_X, ALU.add))
                nc.vector.tensor_scalar(r4[:, a:b], r1[:, a:b], float(CAP), float(FAR), ALU.is_gt, ALU.mult)
                then(nc.vector.tensor_tensor(r2[:, a:b], r2[:, a:b], r1[:, a:b], ALU.add))
                nc.vector.tensor_tensor(slot_i[:, a:b], r2[:, a:b], r4[:, a:b], ALU.add).then_inc(slots_ready, 1)

            first = SPLIT // 4
            lgT_out(first - 1)
            choose(0)
            lgT_out(first)
            slots(0)
            for b in range(first + 1, GBLOCKS):
                lgT_out(b)
            choose(1)
            slots(1)

            for part in (hidh, hidl):
                for f in range(FT):
                    nc.vector.tensor_scalar(part[:, f, USED:], iota_f[:, 0:ESLOT - USED], 0.0, None, ALU.mult).then_inc(pads_done, 1)
            dve.wait_ge(w1h_done, 1)
            nc.vector.tensor_tensor(w1l[:, :, :], we1[:, :, :], w1h[:, :, :].bitcast(F32), ALU.subtract).then_inc(w1l_done, 1)
            dve.wait_ge(w2h_done, 1)
            nc.vector.tensor_tensor(w2l[:, :, :], we2[:, :, :], w2h[:, :, :].bitcast(F32), ALU.subtract).then_inc(w2l_done, 1)

            def in_low(count):
                for h in range(H):
                    dve.wait_ge(inh_done, count - H + h + 1)
                    nc.vector.tensor_tensor(inl[:, h, :], bank[h][:, 0:USED], inh[:, h, :].bitcast(F32), ALU.subtract).then_inc(inl_done, 1)

            def y_pair(i, k, first, p):
                er, m = erest[k], 2 * k + p + 1
                dve.wait_ge(pe_y, i * 4 + m)
                if p == 0:
                    dve.wait_ge(be2_in[k], i * 16 + 16)
                    dve.wait_ge(erest_in[k], i * 16 + 16)
                nc.vector.tensor_tensor(yv, bank[6 + p][:, :].rearrange("p (s d) -> p s d", s=2),
                                        be2[:, k:k + 1, :].broadcast_to([P, 2, D]), ALU.add).then_inc(y_read, 1)
                dve.wait_ge(y_read, i * 4 + m)
                for s in range(2):
                    c = nc.vector.tensor_scalar(yv[:, s, :], yv[:, s, :], er[:, 2 * p + s, D + 1:D + 2], None, ALU.mult)
                c.then_inc(yv_done, 1)
                dve.wait_ge(yv_done, i * 4 + m)
                nc.vector.tensor_scalar(ya, yv, FLT_MAX, NAN_TO_NUM_INF, ALU.is_gt, ALU.mult)
                if not first:
                    for s in range(2 * p, 2 * p + 2):
                        dve.wait_ge(y_sent[s], i * 32 + 16 * k)
                to = yo[:, 2 * p:2 * p + 2, :]
                nc.vector.tensor_scalar(to, yv, -FLT_MAX, -NAN_TO_NUM_INF, ALU.is_lt, ALU.mult).then_inc(y_step, 1)
                dve.wait_ge(y_step, i * 12 + (3 * m - 2))
                nc.vector.tensor_tensor(ya, ya, to, ALU.add).then_inc(y_step, 1)
                dve.wait_ge(y_step, i * 12 + (3 * m - 1))
                dve.wait_ge(mask_done, i * 4 + m)
                dve.sem_inc(dve_go, 1)
                nc.vector.copy_predicated(yv, ymask.bitcast(U32), ya).then_inc(y_step, 1)
                dve.wait_ge(y_step, i * 12 + 3 * m)
                nc.vector.tensor_tensor(to, yv, er[:, 2 * p:2 * p + 2, 0:D], ALU.add).then_inc(y_ready, 1)
                dve.wait_ge(y_ready, i * 4 + m)

            in_low(H)

            def lows_and_y(i, k, first, last):
                if not first:
                    if k:
                        y_pair(i, 0, isinstance(i, int) and i == 0, 1)
                    else:
                        y_pair(i - 1, 1, False, 1)
                for f in range(FT):
                    dve.wait_ge(hidh_done, i * (2 * FT) + (k * FT + f + 1))
                    nc.vector.tensor_tensor(hidl[:, f, 0:USED], hidf[:, f % 4, :], hidh[:, f, 0:USED].bitcast(F32),
                                            ALU.subtract).then_inc(hidl_done, 1)
                if not last:
                    in_low(i * (2 * H) + (k + 2) * H)
                y_pair(i, k, first, 0)
                if last:
                    y_pair(i, k, False, 1)

            experts(dve, lows_and_y)


_INS = ["x", "src", "dst", "edge_weight"] + [f"L0_gnn_{k}" for k in (
    "c1_w1", "c1_b1", "c1_w2", "c1_b2", "c1_g", "c1_b", "bn1_g", "bn1_b",
    "c2_w1", "c2_b1", "c2_w2", "c2_b2", "c2_g", "c2_b", "bn2_g", "bn2_b")] + [
    f"L0_ffn_{k}" for k in ("gate_w", "gate_b", "w1", "b1", "w2", "b2")]


def build(nc, ap, out):
    conv = []
    for l in (1, 2):
        c = {k: ap[f"L0_gnn_c{l}_{k}"] for k in ("w1", "b1", "w2", "b2", "g", "b")}
        c["bng"], c["bnb"] = ap[f"L0_gnn_bn{l}_g"], ap[f"L0_gnn_bn{l}_b"]
        conv.append(c)
    f = {k: ap[f"L0_ffn_{k}"] for k in ("gate_w", "gate_b", "w1", "b1", "w2", "b2")}
    gnn_moe_program(nc, ap["x"], ap["src"], ap["dst"], ap["edge_weight"], conv, f["gate_w"], f["gate_b"],
                    f["w1"], f["b1"], f["w2"], f["b2"], out)


def kernel(**inputs):
    import numpy as _np
    import concourse.bacc as _bacc
    from concourse.bass_utils import run_bass_kernel_spmd as _run

    nc = _bacc.Bacc("TRN2", target_bir_lowering=False, num_devices=1)
    arrays, aps = {}, {}
    for name in _INS:
        a = _np.ascontiguousarray(inputs[name])
        arrays[f"in_{name}"] = a
        aps[name] = nc.dram_tensor(f"in_{name}", a.shape, mybir.dt.from_np(a.dtype), kind="ExternalInput").ap()
    out = nc.dram_tensor("out_x", arrays["in_x"].shape, F32, kind="ExternalOutput").ap()
    build(nc, aps, out)
    r = _run(nc, [arrays], core_ids=[0])
    return r.results[0]["out_x"]
```
